# Optimizing a Trainium2 kernel written in Bass

```python
import numpy as np
import jax
import jax.numpy as jnp

def _softmax(x, axis=-1):
    return jax.nn.softmax(x, axis=axis)

def _gelu(x):
    return jax.nn.gelu(x, approximate=True)

def _silu(x):
    return jax.nn.silu(x)

def _sigmoid(x):
    return jax.nn.sigmoid(x)

def _layernorm(x, axis=-1, eps=1e-05):
    m = jnp.mean(x, axis=axis, keepdims=True)
    v = jnp.var(x, axis=axis, keepdims=True)
    return (x - m) / jnp.sqrt(v + eps)

def _scatter_add(tgt, idx, src, axis=0):
    return tgt.at[idx].add(src)

def _segment_sum(src, seg, n):
    return jax.ops.segment_sum(src, seg, n)
kernel_name = 'mk_cond_seq_d2_seqx_r8_99d3f7'

def setup_inputs(seed: int=0):
    np.random.seed(seed)
    _w = jnp.asarray

    def _rec_inputs():
        import jax
        import jax.numpy as jnp
        _rk = jax.random.key(seed)
        x = -0.0005207 + 1.001 * jax.random.normal(jax.random.fold_in(_rk, 1), (8, 256, 128), jnp.float32)
        _lenS = 256 - jax.random.randint(jax.random.fold_in(_rk, 7), (8,), 0, max(1, 256 // 4) + 1, jnp.int32)
        _lenS2 = 256 - jax.random.randint(jax.random.fold_in(_rk, 8), (8,), 0, max(1, 256 // 4) + 1, jnp.int32)
        itok_B_34_63 = jax.random.randint(jax.random.fold_in(_rk, 12), (8,), 34, 64, jnp.int32)
        fside_Bx16xSxS_0 = -1.47943e-05 + 1.00017 * jax.random.normal(jax.random.fold_in(_rk, 13), (8, 16, 256, 256), jnp.float32)
        itok_B_0_15 = jax.random.randint(jax.random.fold_in(_rk, 14), (8,), 0, 16, jnp.int32)
        _validS = jnp.arange(256)[None, :] < _lenS[:, None]
        _validS2 = jnp.arange(256)[None, :] < _lenS2[:, None]
        _causal = jnp.tril(jnp.ones((256, 256), dtype=bool))
        mask_Bx1xSxS_bk0 = jnp.logical_not(jnp.broadcast_to(_validS[:, None, None, :], (8, 1, 256, 256)))
        return (x, itok_B_34_63, fside_Bx16xSxS_0, itok_B_0_15, mask_Bx1xSxS_bk0)
    x, itok_B_34_63, fside_Bx16xSxS_0, itok_B_0_15, mask_Bx1xSxS_bk0 = _rec_inputs()

    def _L0_cond_setup():
        import jax, jax.numpy as jnp
        import numpy as np
        import math
        D_MODEL = 128
        N_HEAD = 16
        HEAD_DIM = D_MODEL // N_HEAD
        D_FF = 512
        NUM_STEPS = 100.0
        RESCALE = 4000.0
        EPS = 1e-05

        def _sin_emb(t):
            half = D_MODEL // 2
            x = t.astype(jnp.float32) / NUM_STEPS * RESCALE
            freqs = jnp.exp(jnp.arange(half, dtype=jnp.float32) * (-math.log(10000.0) / (half - 1)))
            e = x[:, None] * freqs[None, :]
            return jnp.concatenate([jnp.sin(e), jnp.cos(e)], axis=-1)

        def _ln(x):
            m = jnp.mean(x, axis=-1, keepdims=True)
            v = jnp.var(x, axis=-1, keepdims=True)
            return (x - m) / jnp.sqrt(v + EPS)

        def _gelu2(x):
            return x * jax.nn.sigmoid(1.702 * x)
        key = jax.random.key(seed)
        ks = jax.random.split(key, 24)
        B, S, D, F = (4, 64, D_MODEL, D_FF)
        std = 0.02
        inp = {'src': jax.random.normal(ks[0], (B, S, D), dtype=jnp.float32), 'src_mask': jax.random.randint(ks[1], (B, 1, S, S), 0, 2).astype(bool), 'timestep': jax.random.randint(ks[2], (B,), 0, 100, dtype=jnp.int32), 'attention_bias': jax.random.normal(ks[3], (B, N_HEAD, S, S), dtype=jnp.float32), 'W_ada': jax.random.normal(ks[4], (D, 2 * D), dtype=jnp.float32) * std, 'b_ada': jnp.zeros((2 * D,), dtype=jnp.float32), 'Wq': jax.random.normal(ks[5], (D, D), dtype=jnp.float32) * std, 'bq': jnp.zeros((D,), dtype=jnp.float32), 'Wk': jax.random.normal(ks[6], (D, D), dtype=jnp.float32) * std, 'bk': jnp.zeros((D,), dtype=jnp.float32), 'Wv': jax.random.normal(ks[7], (D, D), dtype=jnp.float32) * std, 'bv': jnp.zeros((D,), dtype=jnp.float32), 'Wo': jax.random.normal(ks[8], (D, D), dtype=jnp.float32) * std, 'bo': jnp.zeros((D,), dtype=jnp.float32), 'W1': jax.random.normal(ks[9], (D, F), dtype=jnp.float32) * std, 'b1': jnp.zeros((F,), dtype=jnp.float32), 'W2': jax.random.normal(ks[10], (F, D), dtype=jnp.float32) * std, 'b2': jnp.zeros((D,), dtype=jnp.float32), 'g2': jnp.ones((D,), dtype=jnp.float32), 'beta2': jnp.zeros((D,), dtype=jnp.float32)}
        return inp
    _L0_cond_all = _L0_cond_setup()
    _L0_cond_in = {k: v for k, v in _L0_cond_all.items() if k in ('W_ada', 'b_ada', 'Wq', 'bq', 'Wk', 'bk', 'Wv', 'bv', 'Wo', 'bo', 'W1', 'b1', 'W2', 'b2', 'g2', 'beta2')}
    del _L0_cond_all

    def _L1_cond_setup():
        import jax, jax.numpy as jnp
        import numpy as np
        B, S, D = (32, 128, 128)
        A = 32
        E = 16
        LN_EPS = 1e-05
        key = jax.random.key(seed)
        ks = jax.random.split(key, 10)
        s = lambda fan_in: 1.0 / np.sqrt(fan_in)
        return {'hidden_states': jax.random.normal(ks[0], (B, S, D), dtype=jnp.float32), 'domain_id': jax.random.randint(ks[1], (B,), 0, E, dtype=jnp.int64), 'down_W': jax.random.uniform(ks[2], (A, D), jnp.float32, -s(D), s(D)), 'down_b': jax.random.uniform(ks[3], (A,), jnp.float32, -s(D), s(D)), 'up_W': jax.random.uniform(ks[4], (D, A), jnp.float32, -s(A), s(A)), 'up_b': jax.random.uniform(ks[5], (D,), jnp.float32, -s(A), s(A)), 'expert_W': jax.random.uniform(ks[6], (E, A, A), jnp.float32, -s(A), s(A)), 'expert_b': jax.random.uniform(ks[7], (E, A), jnp.float32, -s(A), s(A)), 'domain_emb': jax.random.normal(ks[8], (E, A), dtype=jnp.float32), 'ln_gamma': jnp.ones((D,), jnp.float32), 'ln_beta': jnp.zeros((D,), jnp.float32)}
    _L1_cond_all = _L1_cond_setup()
    _L1_cond_in = {k: v for k, v in _L1_cond_all.items() if k in ('down_W', 'down_b', 'up_W', 'up_b', 'expert_W', 'expert_b', 'domain_emb', 'ln_gamma', 'ln_beta')}
    del _L1_cond_all
    return {'x': x, 'itok_B_34_63': itok_B_34_63, 'fside_Bx16xSxS_0': fside_Bx16xSxS_0, 'itok_B_0_15': itok_B_0_15, 'mask_Bx1xSxS_bk0': mask_Bx1xSxS_bk0, 'L0_cond_W_ada': _L0_cond_in['W_ada'], 'L0_cond_b_ada': _L0_cond_in['b_ada'], 'L0_cond_Wq': _L0_cond_in['Wq'], 'L0_cond_bq': _L0_cond_in['bq'], 'L0_cond_Wk': _L0_cond_in['Wk'], 'L0_cond_bk': _L0_cond_in['bk'], 'L0_cond_Wv': _L0_cond_in['Wv'], 'L0_cond_bv': _L0_cond_in['bv'], 'L0_cond_Wo': _L0_cond_in['Wo'], 'L0_cond_bo': _L0_cond_in['bo'], 'L0_cond_W1': _L0_cond_in['W1'], 'L0_cond_b1': _L0_cond_in['b1'], 'L0_cond_W2': _L0_cond_in['W2'], 'L0_cond_b2': _L0_cond_in['b2'], 'L0_cond_g2': _L0_cond_in['g2'], 'L0_cond_beta2': _L0_cond_in['beta2'], 'L1_cond_down_W': _L1_cond_in['down_W'], 'L1_cond_down_b': _L1_cond_in['down_b'], 'L1_cond_up_W': _L1_cond_in['up_W'], 'L1_cond_up_b': _L1_cond_in['up_b'], 'L1_cond_expert_W': _L1_cond_in['expert_W'], 'L1_cond_expert_b': _L1_cond_in['expert_b'], 'L1_cond_domain_emb': _L1_cond_in['domain_emb'], 'L1_cond_ln_gamma': _L1_cond_in['ln_gamma'], 'L1_cond_ln_beta': _L1_cond_in['ln_beta']}

def reference(x, itok_B_34_63, fside_Bx16xSxS_0, itok_B_0_15, mask_Bx1xSxS_bk0, L0_cond_W_ada, L0_cond_b_ada, L0_cond_Wq, L0_cond_bq, L0_cond_Wk, L0_cond_bk, L0_cond_Wv, L0_cond_bv, L0_cond_Wo, L0_cond_bo, L0_cond_W1, L0_cond_b1, L0_cond_W2, L0_cond_b2, L0_cond_g2, L0_cond_beta2, L1_cond_down_W, L1_cond_down_b, L1_cond_up_W, L1_cond_up_b, L1_cond_expert_W, L1_cond_expert_b, L1_cond_domain_emb, L1_cond_ln_gamma, L1_cond_ln_beta):
    import jax
    import jax.numpy as jnp

    def _L0_cond_ref(src, src_mask, timestep, attention_bias, W_ada, b_ada, Wq, bq, Wk, bk, Wv, bv, Wo, bo, W1, b1, W2, b2, g2, beta2):
        import jax, jax.numpy as jnp
        import numpy as np
        import math
        D_MODEL = 128
        N_HEAD = 16
        HEAD_DIM = D_MODEL // N_HEAD
        D_FF = 512
        NUM_STEPS = 100.0
        RESCALE = 4000.0
        EPS = 1e-05

        def _sin_emb(t):
            half = D_MODEL // 2
            x = t.astype(jnp.float32) / NUM_STEPS * RESCALE
            freqs = jnp.exp(jnp.arange(half, dtype=jnp.float32) * (-math.log(10000.0) / (half - 1)))
            e = x[:, None] * freqs[None, :]
            return jnp.concatenate([jnp.sin(e), jnp.cos(e)], axis=-1)

        def _ln(x):
            m = jnp.mean(x, axis=-1, keepdims=True)
            v = jnp.var(x, axis=-1, keepdims=True)
            return (x - m) / jnp.sqrt(v + EPS)

        def _gelu2(x):
            return x * jax.nn.sigmoid(1.702 * x)
        B, S, D = src.shape
        emb = jax.nn.silu(_sin_emb(timestep)) @ W_ada + b_ada
        scale, shift = jnp.split(emb[:, None, :], 2, axis=-1)
        x = _ln(src) * (1.0 + scale) + shift
        q = (x @ Wq + bq).reshape(B, S, N_HEAD, HEAD_DIM).transpose(0, 2, 1, 3)
        k = (x @ Wk + bk).reshape(B, S, N_HEAD, HEAD_DIM).transpose(0, 2, 1, 3)
        v = (x @ Wv + bv).reshape(B, S, N_HEAD, HEAD_DIM).transpose(0, 2, 1, 3)
        scores = jnp.einsum('bhqd,bhkd->bhqk', q / math.sqrt(HEAD_DIM), k)
        scores = scores + attention_bias
        scores = jnp.where(src_mask, -jnp.inf, scores.astype(jnp.float32))
        probs = jax.nn.softmax(scores, axis=-1).astype(v.dtype)
        ctx = jnp.einsum('bhqk,bhkd->bhqd', probs, v)
        ctx = ctx.transpose(0, 2, 1, 3).reshape(B, S, D)
        x = x + (ctx @ Wo + bo)
        h = _ln(x) * g2 + beta2
        ff = _gelu2(h @ W1 + b1) @ W2 + b2
        return x + ff

    def _L1_cond_ref(hidden_states, domain_id, down_W, down_b, up_W, up_b, expert_W, expert_b, domain_emb, ln_gamma, ln_beta):
        import jax, jax.numpy as jnp
        import numpy as np
        B, S, D = (32, 128, 128)
        A = 32
        E = 16
        LN_EPS = 1e-05
        residual = hidden_states
        hidden = jnp.einsum('bsd,ad->bsa', hidden_states, down_W) + down_b
        hidden = jax.nn.gelu(hidden, approximate=False)
        valid = (domain_id >= 0) & (domain_id < E)
        idx = jnp.clip(domain_id, 0, E - 1)
        Wsel = expert_W[idx]
        bsel = expert_b[idx]
        expert_out = jnp.einsum('bsa,boa->bso', hidden, Wsel) + bsel[:, None, :]
        domain_output = jnp.where(valid[:, None, None], expert_out, hidden)
        hidden = domain_output + domain_emb[idx][:, None, :]
        hidden = jnp.einsum('bsa,da->bsd', hidden, up_W) + up_b
        x = hidden + residual
        mu = jnp.mean(x, axis=-1, keepdims=True)
        var = jnp.mean(jnp.square(x - mu), axis=-1, keepdims=True)
        return (x - mu) * jax.lax.rsqrt(var + LN_EPS) * ln_gamma + ln_beta
    x = _L0_cond_ref(x, mask_Bx1xSxS_bk0, itok_B_34_63, fside_Bx16xSxS_0, L0_cond_W_ada, L0_cond_b_ada, L0_cond_Wq, L0_cond_bq, L0_cond_Wk, L0_cond_bk, L0_cond_Wv, L0_cond_bv, L0_cond_Wo, L0_cond_bo, L0_cond_W1, L0_cond_b1, L0_cond_W2, L0_cond_b2, L0_cond_g2, L0_cond_beta2)
    x = _L1_cond_ref(x, itok_B_0_15, L1_cond_down_W, L1_cond_down_b, L1_cond_up_W, L1_cond_up_b, L1_cond_expert_W, L1_cond_expert_b, L1_cond_domain_emb, L1_cond_ln_gamma, L1_cond_ln_beta)
    return x

_drawn_inputs = setup_inputs


def setup_inputs(seed=0):
    import zlib

    import numpy as np

    out = dict(_drawn_inputs(seed))
    spreads = {'L0_cond_b_ada': (0.0, 0.1),
     'L0_cond_bq': (0.0, 0.8),
     'L0_cond_bk': (0.0, 0.8),
     'L0_cond_bv': (0.0, 0.469),
     'L0_cond_bo': (0.0, 0.1),
     'L0_cond_b1': (0.0, 0.386),
     'L0_cond_b2': (0.0, 0.1),
     'L0_cond_g2': (1.0, 0.6),
     'L0_cond_beta2': (0.0, 0.8),
     'L1_cond_ln_gamma': (1.0, 0.2),
     'L1_cond_ln_beta': (0.0, 0.1)}
    factors = {'fside_Bx16xSxS_0': 8.0,
     'L0_cond_Wq': 8.0,
     'L0_cond_Wk': 8.0,
     'L0_cond_Wv': 7.47,
     'L0_cond_Wo': 2.944,
     'L1_cond_down_b': 6.011}
    for name, (base, spread) in spreads.items():
        noise = np.random.default_rng([zlib.crc32(name.encode()), seed]).standard_normal(out[name].shape)
        drawn = base * np.exp(spread * noise) if base else spread * noise
        out[name] = jnp.asarray(drawn.astype(out[name].dtype))
    for name, factor in factors.items():
        out[name] = (out[name] * factor).astype(out[name].dtype)
    return out
```

```python
import concourse.bass as bass
from concourse import mybir
from contextlib import ExitStack


def cond_seq_kernel(nc, x, tstep, fside, domain, mask, wts, cols, rows, bo, down, up, expert,
                    identf, identb, negsel, out):
    fp32 = mybir.dt.float32
    bf16 = mybir.dt.bfloat16
    i32 = mybir.dt.int32
    u8 = mybir.dt.uint8
    ALU = mybir.AluOpType
    ACT = mybir.ActivationFunctionType

    B, S, D = x.shape
    H = fside.shape[1]
    HD = D // H
    P = 128
    QT = S // P
    FF = 4
    A = down.shape[1]
    NE = 16
    G = 4
    NG = H // G
    QS = float(HD) ** -0.5
    EPS = 1e-5
    MASKED = -3.0e38
    RING = 8
    NPT = 8
    NPARTS = 3
    KROWS = NPARTS * NPARTS * HD
    LAG = 20
    TAU1 = 6.28125
    TAU2 = 0.0019350051879882812
    TAU3 = 6.283185307179586 - TAU1 - TAU2
    RESCALE, STEPS_T = 4000.0, 100.0
    ROUND = 12582912.0
    MAGIC = float(0x5F3759DF)

    parts_dram = nc.dram_tensor("parts_dram", [2, 2, HD, NPARTS, H, S], bf16).ap()

    ctx = ExitStack()
    with ctx:
        def sb(name, shape, dt=fp32):
            return ctx.enter_context(nc.sbuf_tensor(name, shape, dt))

        def sem(name):
            return ctx.enter_context(nc.semaphore(name))

        wts_sb = sb("wts_sb", [P, wts.shape[1]])
        WQ, WK, WV, WO = (wts_sb[:, i * D:(i + 1) * D] for i in range(4))
        WADA = wts_sb[:, 4 * D:6 * D]
        W1 = wts_sb[:, 6 * D:6 * D + FF * P]
        W2 = wts_sb[:, 6 * D + FF * P:6 * D + 2 * FF * P]
        cols_sb = sb("cols_sb", [P, cols.shape[1]])
        (BADA_S, BADA_H, BQ, BK, G2, BETA2, B2, FREQ, PHASE, ECOL, DOWNB) = range(11)
        B1 = 11

        def col(i, n=1, p=P):
            return cols_sb[0:p, i:i + n]

        rows_sb = sb("rows_sb", [P, 3, D])
        bo_sb = sb("bo_sb", [1, D])
        down_sb = sb("down_sb", [P, A])
        up_sb = sb("up_sb", [A + 1, D])
        idf = sb("idf", [P, P])
        idb = sb("idb", [P, P], bf16)
        negsel_sb = sb("negsel_sb", [96, H, P], bf16)
        ones_row = sb("ones_row", [1, P])

        x_sb = sb("x_sb", [P, B, QT, D])
        st1 = sb("st1", [P, B * QT, 6])
        mv1 = sb("mv1", [P, B * QT, 2])
        nt1 = sb("nt1", [P, 4, B * QT])
        z1 = sb("z1", [P, 2, QT, D])
        x1T = sb("x1T", [P, B, S])
        qkf = sb("qkf", [P, 2, S])
        parts = sb("parts", [P, 2, NPARTS, S], bf16)
        qk_rest = sb("qk_rest", [P, 2, S])
        qstack = sb("qstack", [KROWS, 2, H, S], bf16)
        kstack = sb("kstack", [KROWS, 2, H, S], bf16)
        vaug = sb("vaug", [P, 2, QT, H, 32])
        mask_sb = sb("mask_sb", [P, 2, QT, S], u8)
        maskb = sb("maskb", [P, 2, QT, S], bf16)
        F = sb("F", [P, RING, G, QT, S])
        mx = sb("mx", [P, 2, QT, H])
        mrep = sb("mrep", [P, 2, QT, NPARTS, 32])
        nanfix = sb("nanfix", [P, 2, QT, H])
        mT = sb("mT", [96, S])
        m_rest = sb("m_rest", [96, S])
        mstack = sb("mstack", [96, 2, S], bf16)
        PT = sb("PT", [P, NPT, QT, S])
        ctxA = sb("ctxA", [P, NG, S])
        csum = sb("csum", [P, QT, H])
        ctxn = sb("ctxn", [P, QT, D])
        ctxT = sb("ctxT", [P, S])
        x2 = sb("x2", [P, 2, QT, D])
        st2 = sb("st2", [P, QT, 6])
        mv2 = sb("mv2", [P, 2, QT, 2])
        nt2 = sb("nt2", [P, 4, QT])
        z2 = sb("z2", [P, QT, D])
        hT = sb("hT", [P, S])
        u = sb("u", [P, FF, S])
        th = sb("th", [P, FF, S])
        x3T = sb("x3T", [P, B, S])
        hid = sb("hid", [A, B, S])
        ghid = hid
        expert_sb = PT[0:A + 1, :, :, :].rearrange("p n t s -> p (n t s)")[:, 0:expert.shape[1]]
        eoT = PT[0:A + 1, 0:4, :, :].rearrange("p n t s -> p (n t) s")
        emb = sb("emb", [P, 8, B])
        emb_i = sb("emb_i", [P, B], i32)
        dom_i = sb("dom_i", [A + 1, B], i32)
        dom = sb("dom", [A + 1, 6, B])
        ada = sb("ada", [P, 2, B])
        qbias = sb("qbias", [P, 1])
        wsel = sb("wsel", [A, B, A])
        bsel = sb("bsel", [A, B])
        st3 = sb("st3", [P, B * QT, 6])
        mv3 = sb("mv3", [P, B * QT, 2])
        nt3 = sb("nt3", [P, 4, B * QT])
        y = x_sb

        banks = [ctx.enter_context(nc.psum_tensor(f"bank{i}", [P, 512], fp32)) for i in range(8)]
        SB = banks[0:2]
        ZB = banks[2:4]
        CB = banks[4]
        MA, MB, MC = banks[5:8]

        EB = [MA, CB, *ZB]
        UB = [MB, MC, *SB]

        names = """w_in cols_in rows_in bo_in down_in up_in expert_in idf_in idb_in sel_in
            t_in dom_in ones_set pads_set
            emb_x emb_sin emb_exp emb_silu ada_mm ada_ready dom_ready wsel_mm wsel_ready
            stats1 y1_seed nt1_step z1_ready t1_done x1T_ready qkp_done qk_ready split_step parts_ready
            parts_out vp_done v_ready maskb_ready scores_done scores_read mrep_ready tm_done
            mT_ready msplit_step nan_ready turned probs_ready ctx_done ctxA_ready tc_done rsum_fixed rsum_inv
            ctxn_ready tc2_done ctxT_ready o_done x2_ready stats2 y2_seed nt2_step z2_ready
            t2_done hT_ready ff1_done u_ready th_ready g_ready ff2_done x3_ready dn_done hid_ready
            ghid_ready eo_done eo_ready up_done st3_step y3_seed nt3_step norm3_ready z3_ready y_ready
            out_done""".split()
        sm = {n: sem(n) for n in names}
        x_in = [sem(f"x_in{i}") for i in range(B)]
        mask_in = [sem(f"mask_in{i}") for i in range(2)]
        f_in = [sem(f"f_in{i}") for i in range(RING)]
        q_in = [sem(f"q_in{i}") for i in range(2)]
        k_in = [sem(f"k_in{i}") for i in range(2)]

        block = ctx.enter_context(nc.Block())
        STEPS = range(-1, B + 2)

        def item(n, back):
            return n - back if 0 <= n - back < B else None

        def turning(n, h):
            s = H * n + h - LAG
            return (s // H, s % H) if 0 <= s < B * H else None

        def using(n, h):
            s = H * n + h - LAG - (G - 1) - 2
            return (s // H, s % H // G) if 0 <= s < B * H and s % G == 0 else None

        def newton_seed(dve, mv, nt, stats_sem, seed_sem, v0, s0, n):
            dve.wait_ge(stats_sem, v0)
            nc.vector.tensor_scalar(nt[:, 2, :], mv, EPS, None, ALU.add).then_inc(seed_sem, 1)
            dve.wait_ge(seed_sem, s0 + 1)
            nc.vector.tensor_scalar(nt[:, 0, :], nt[:, 2, :], -0.5, None, ALU.mult).then_inc(seed_sem, 1)
            nc.vector.tensor_scalar(nt[:, 3, :].bitcast(i32), nt[:, 2, :].bitcast(i32), 1, None,
                                    ALU.logical_shift_right).then_inc(seed_sem, 1)
            dve.wait_ge(seed_sem, s0 + 3)
            nc.vector.tensor_scalar(nt[:, 1, :].bitcast(i32), nt[:, 3, :].bitcast(i32), -1.0, MAGIC,
                                    ALU.mult, ALU.add).then_inc(seed_sem, 1)

        def newton_steps(eng, nt, seed_sem, s0, step_sem, k0):
            eng.wait_ge(seed_sem, s0)
            k = k0
            for r in range(4):
                if r:
                    eng.wait_ge(step_sem, k)
                eng.tensor_tensor(out=nt[:, 2, :], in0=nt[:, 1, :], in1=nt[:, 1, :],
                                  op=ALU.mult).then_inc(step_sem, 1)
                eng.wait_ge(step_sem, k + 1)
                eng.tensor_tensor(out=nt[:, 3, :], in0=nt[:, 2, :], in1=nt[:, 0, :],
                                  op=ALU.mult).then_inc(step_sem, 1)
                eng.wait_ge(step_sem, k + 2)
                eng.tensor_scalar(nt[:, 2, :], nt[:, 3, :], 1.0, 1.5, ALU.mult, ALU.add).then_inc(step_sem, 1)
                eng.wait_ge(step_sem, k + 3)
                eng.tensor_tensor(out=nt[:, 1, :], in0=nt[:, 1, :], in1=nt[:, 2, :],
                                  op=ALU.mult).then_inc(step_sem, 1)
                k += 4
        NSTEP = 16
        NSEED = 4

        @block.sync
        def _(sp):
            def load_x(b):
                sp.dma_start(x_sb[:, b, :, :], x[b].rearrange("(t p) d -> p t d", p=P)).then_inc(x_in[b], 16)

            def load_mask(b):
                if b >= 2:
                    sp.wait_ge(sm["maskb_ready"], b - 1)
                sp.dma_start(mask_sb[:, b % 2, :, :],
                             mask[b, 0].rearrange("(t p) k -> p t k", p=P)).then_inc(mask_in[b % 2], 16)

            def load_bias(b, g):
                r = (b * NG + g) % RING
                if b >= 2:
                    sp.wait_ge(sm["turned"], H * (b - 2) + G * (g + 1))
                sp.dma_start(F[:, r, :, :, :],
                             fside[b, G * g:G * (g + 1)].rearrange("h (t p) k -> p h t k", p=P)
                             ).then_inc(f_in[r], 16)

            load_x(0)
            sp.dma_start(idf[:, :], identf).then_inc(sm["idf_in"], 16)
            sp.dma_start(cols_sb[:, :], cols).then_inc(sm["cols_in"], 16)
            sp.dma_start(emb_i[:, :], tstep.rearrange("(o b) -> o b", o=1).to_broadcast([P, B])
                         ).then_inc(sm["t_in"], 16)
            sp.dma_start(wts_sb[:, :], wts).then_inc(sm["w_in"], 16)
            sp.dma_start(rows_sb[:, :, :], rows.rearrange("(o r) d -> o r d", o=1).to_broadcast([P, 3, D])
                         ).then_inc(sm["rows_in"], 16)
            load_mask(0)
            sp.dma_start(idb[:, :], identb).then_inc(sm["idb_in"], 16)
            for b in range(1, B):
                load_x(b)
            load_bias(0, 0)
            load_bias(0, 1)
            sp.dma_start(negsel_sb[:, :, :], negsel).then_inc(sm["sel_in"], 16)
            sp.dma_start(bo_sb[:, :], bo).then_inc(sm["bo_in"], 16)
            sp.dma_start(dom_i[:, :], domain.rearrange("(o b) -> o b", o=1).to_broadcast([A + 1, B])
                         ).then_inc(sm["dom_in"], 16)
            sp.dma_start(down_sb[:, :], down).then_inc(sm["down_in"], 16)
            sp.dma_start(up_sb[:, :], up).then_inc(sm["up_in"], 16)
            sp.dma_start(expert_sb, expert).then_inc(sm["expert_in"], 16)

            for n in STEPS:
                c = item(n, 0)
                if c is not None:
                    load_bias(c, 3)
                b = item(n, -1)
                if b is None:
                    continue
                if b >= 1:
                    load_mask(b)
                    load_bias(b, 0)
                    load_bias(b, 1)
                sp.wait_ge(sm["parts_ready"], 2 * (b + 1))
                if b >= 1:
                    sp.wait_ge(q_in[(b - 1) % 2], 16 * ((b - 1) // 2 + 1))
                for w in range(2):
                    for i in range(NPARTS):
                        sp.dma_start(parts_dram[b % 2, w, :, i].rearrange("d h s -> h d s"),
                                     parts[:, w, i, :]).then_inc(sm["parts_out"], 16)
                sp.wait_ge(sm["parts_out"], 16 * 2 * NPARTS * (b + 1))
                if b >= 2:
                    sp.wait_ge(sm["scores_done"], H * (b - 1))
                pq = parts_dram[b % 2, 0].rearrange("d i h s -> (d i) (h s)")
                pk = parts_dram[b % 2, 1].rearrange("d j h s -> j d (h s)")
                sp.dma_start(qstack[:, b % 2, :, :].rearrange("p h s -> p (h s)"),
                             pq.unsqueeze(1).to_broadcast([HD * NPARTS, NPARTS, H * S])
                             ).then_inc(q_in[b % 2], 16)
                for j in range(NPARTS):
                    sp.dma_start(kstack[j::NPARTS, b % 2, :, :].rearrange("p h s -> p (h s)"),
                                 pk[j].unsqueeze(1).to_broadcast([HD, NPARTS, H * S])
                                 ).then_inc(k_in[b % 2], 16)
                load_bias(b, 2)

            for b in range(B):
                sp.wait_ge(sm["y_ready"], b + 1)
                sp.dma_start(out[b].rearrange("(t p) d -> p t d", p=P), y[:, b, :, :]).then_inc(sm["out_done"], 16)
            sp.wait_ge(sm["out_done"], 16 * B)

        @block.gpsimd
        def _(pool):
            pool.memset(ones_row[:, :], 1.0)
            pool.memset(mrep[:, :, :, :, :], 0.0).then_inc(sm["pads_set"], 1)
            newton_steps(pool, nt1[:, :, 0:QT], sm["y1_seed"], NSEED, sm["nt1_step"], 0)
            rest_done = False

            def mask_bias(b):
                pool.wait_ge(mask_in[b % 2], 16 * (b // 2 + 1))
                if b >= 2:
                    pool.wait_ge(sm["scores_done"], H * (b - 1))
                pool.tensor_scalar(maskb[:, b % 2, :, :], mask_sb[:, b % 2, :, :], MASKED, None,
                                   ALU.mult).then_inc(sm["maskb_ready"], 1)

            for n in STEPS:
                c = item(n, 1)
                if c is not None:
                    pool.wait_ge(sm["scores_read"], H * (c + 1))
                    pool.wait_ge(sm["pads_set"], 1)
                    if c >= 2:
                        pool.wait_ge(sm["tm_done"], c - 1)
                        pool.wait_ge(sm["rsum_fixed"], c - 1)
                    for t in range(QT):
                        last = pool.tensor_scalar(
                            mrep[:, c % 2, t, :, 0:H],
                            mx[:, c % 2, t:t + 1, :].to_broadcast([P, NPARTS, H]), 1.0, None, ALU.mult)
                    last.then_inc(sm["mrep_ready"], 1)
                    pool.tensor_scalar(nanfix[:, c % 2, :, :], mx[:, c % 2, :, :], 2.0, 0.0,
                                       ALU.mult, ALU.mult).then_inc(sm["nan_ready"], 1)
                    pool.wait_ge(sm["mT_ready"], c + 1)
                    if c >= 2:
                        pool.wait_ge(sm["turned"], H * (c - 1))
                    ms = mstack[:, c % 2, :]
                    pool.tensor_scalar(ms, mT[:, :], 1.0, None, ALU.mult).then_inc(sm["msplit_step"], 1)
                    pool.wait_ge(sm["msplit_step"], 4 * c + 1)
                    pool.tensor_tensor(out=m_rest[:, :], in0=mT[:, :], in1=ms, op=ALU.subtract
                                       ).then_inc(sm["msplit_step"], 1)
                    pool.wait_ge(sm["msplit_step"], 4 * c + 2)
                    pool.tensor_scalar(ms[0:64, :], m_rest[0:64, :], 1.0, None, ALU.mult
                                       ).then_inc(sm["msplit_step"], 1)
                    pool.wait_ge(sm["msplit_step"], 4 * c + 3)
                    pool.tensor_tensor(out=ms[0:32, :], in0=m_rest[0:32, :], in1=ms[0:32, :],
                                       op=ALU.subtract).then_inc(sm["msplit_step"], 1)
                b = item(n, -1)
                if b is not None:
                    mask_bias(b)
                    pool.wait_ge(sm["qk_ready"], 2 * (b + 1))
                    if b >= 1:
                        pool.wait_ge(sm["parts_out"], 16 * 2 * NPARTS * b)
                    pool.tensor_scalar(parts[:, :, 0, :], qkf[:, :, :], 1.0, None, ALU.mult
                                       ).then_inc(sm["split_step"], 1)
                    pool.wait_ge(sm["split_step"], 3 * b + 1)
                    pool.tensor_tensor(out=qk_rest[:, :, :], in0=qkf[:, :, :], in1=parts[:, :, 0, :],
                                       op=ALU.subtract).then_inc(sm["split_step"], 1)
                    pool.wait_ge(sm["split_step"], 3 * b + 2)
                    pool.tensor_scalar(parts[:, :, 1, :], qk_rest[:, :, :], 1.0, None, ALU.mult
                                       ).then_inc(sm["split_step"], 1)
                    pool.wait_ge(sm["split_step"], 3 * b + 3)
                    for w in range(2):
                        pool.tensor_tensor(out=parts[:, w, 2, :], in0=qk_rest[:, w, :],
                                           in1=parts[:, w, 1, :], op=ALU.subtract
                                           ).then_inc(sm["parts_ready"], 1)
                if not rest_done:
                    newton_steps(pool, nt1[:, :, QT:], sm["y1_seed"], 2 * NSEED, sm["nt1_step"], NSTEP)
                    rest_done = True
                c = item(n, 2)
                if c is not None:
                    newton_steps(pool, nt2, sm["y2_seed"], NSEED * (c + 1), sm["nt2_step"], NSTEP * c)
            pool.wait_ge(sm["ctx_done"], NG * B)
            pool.wait_ge(sm["nt2_step"], NSTEP * B)
            pool.memset(eoT[A:A + 1, :, :], 1.0).then_inc(sm["pads_set"], 1)
            pool.wait_ge(sm["pads_set"], 2)
            for b in range(B):
                pool.wait_ge(sm["z3_ready"], 2 * (b + 1) - 1)
                pool.tensor_tensor(out=y[:, b, 0, :], in0=y[:, b, 0, :], in1=rows_sb[:, 2, :],
                                   op=ALU.add)
                pool.wait_ge(sm["z3_ready"], 2 * (b + 1))
                pool.tensor_tensor(out=y[:, b, 1, :], in0=y[:, b, 1, :], in1=rows_sb[:, 2, :],
                                   op=ALU.add).then_inc(sm["y_ready"], 1)

        @block.scalar
        def _(act):
            act.wait_ge(sm["emb_x"], 6)
            nc.scalar.activation(emb[:, 3, :], emb[:, 2, :], ACT.Sin).then_inc(sm["emb_sin"], 1)
            act.wait_ge(sm["emb_sin"], 1)
            nc.scalar.activation(emb[:, 4, :], emb[:, 3, :], ACT.Exp, scale=-1.0).then_inc(sm["emb_exp"], 1)
            act.wait_ge(sm["cols_in"], 16)
            nc.scalar.activation(qbias[:, :], col(BQ), ACT.Copy, scale=QS)

            def x1T_out(b):
                act.wait_ge(sm["t1_done"], b + 1)
                act.wait_ge(sm["ada_ready"], 2)
                nc.scalar.activation(x1T[:, b, :], MA[:, 0:S], ACT.Identity, bias=ada[:, 1, b:b + 1],
                                     scale=ada[:, 0, b:b + 1]).then_inc(sm["x1T_ready"], 1)

            def qk_out(b):
                act.wait_ge(sm["qkp_done"], b + 1)
                if b >= 1:
                    act.wait_ge(sm["parts_ready"], 2 * b)
                nc.scalar.activation(qkf[:, 0, :], MA[:, 0:S], ACT.Identity, bias=qbias[:, :], scale=QS
                                     ).then_inc(sm["qk_ready"], 1)
                nc.scalar.activation(qkf[:, 1, :], MA[:, S:2 * S], ACT.Identity, bias=col(BK)
                                     ).then_inc(sm["qk_ready"], 1)

            def mT_out(c):
                act.wait_ge(sm["tm_done"], c + 1)
                if c >= 1:
                    act.wait_ge(sm["msplit_step"], 4 * c)
                nc.scalar.activation(mT[:, :], MA[0:96, 0:S], ACT.Copy).then_inc(sm["mT_ready"], 1)

            def probs(c, h):
                k = H * c + h
                act.wait_ge(sm["turned"], k + 1)
                if k == 0:
                    act.wait_ge(sm["wsel_mm"], 1)
                if k >= NPT:
                    act.wait_ge(sm["ctx_done"], (k - NPT) // G + 1)
                nc.scalar.activation(PT[:, k % NPT, :, :], ZB[k % 2][:, :].rearrange("p (t q) -> p t q", t=QT),
                                     ACT.Exp).then_inc(sm["probs_ready"], 1)

            def ctxA_out(c, j):
                act.wait_ge(sm["ctx_done"], NG * c + 2 * (j + 1))
                if c >= 1:
                    act.wait_ge(sm["tc_done"], 2 * c)
                nc.scalar.activation(ctxA[:, 2 * j:2 * j + 2, :],
                                     CB[:, :].rearrange("p (g q) -> p g q", g=2), ACT.Copy
                                     ).then_inc(sm["ctxA_ready"], 1)

            def ctxT_out(c):
                act.wait_ge(sm["tc2_done"], c + 1)
                if c >= 1:
                    act.wait_ge(sm["o_done"], c)
                nc.scalar.activation(ctxT[:, :], MB[:, 0:S], ACT.Copy).then_inc(sm["ctxT_ready"], 1)

            def x2_out(c):
                act.wait_ge(sm["o_done"], c + 1)
                if c >= 2:
                    act.wait_ge(sm["ff2_done"], c - 1)
                nc.scalar.activation(x2[:, c % 2, :, :], MC[:, 0:S].rearrange("p (t d) -> p t d", t=QT),
                                     ACT.Copy).then_inc(sm["x2_ready"], 1)

            def hT_out(c):
                act.wait_ge(sm["t2_done"], c + 1)
                if c >= 1:
                    act.wait_ge(sm["ff1_done"], 2 * c)
                nc.scalar.activation(hT[:, :], MB[:, S:2 * S], ACT.Identity, bias=col(BETA2), scale=col(G2)
                                     ).then_inc(sm["hT_ready"], 1)

            def th_out(c, j):
                act.wait_ge(sm["u_ready"], 2 * c + j + 1)
                if c >= 1:
                    act.wait_ge(sm["g_ready"], 2 * (c - 1) + j + 1)
                nc.scalar.activation(th[:, 2 * j:2 * j + 2, :], u[:, 2 * j:2 * j + 2, :], ACT.Tanh,
                                     scale=0.851).then_inc(sm["th_ready"], 1)

            def x3_out(c):
                act.wait_ge(sm["ff2_done"], c + 1)
                nc.scalar.activation(x3T[:, c, :], MB[:, 0:S], ACT.Identity, bias=col(B2)
                                     ).then_inc(sm["x3_ready"], 1)

            def hid_out(c):
                act.wait_ge(sm["dn_done"], c + 1)
                nc.scalar.activation(hid[:, c, :], MC[0:A, 0:S], ACT.Identity, bias=col(DOWNB, 1, A)
                                     ).then_inc(sm["hid_ready"], 1)

            table = {1: [(mT_out, 1), (x3_out, 3)], 3: [(x1T_out, -1), (hid_out, 3)], 5: [(qk_out, -1)],
                     9: [(ctxT_out, 2)], 11: [(x2_out, 2)], 13: [(hT_out, 2)],
                     14: [(lambda c: th_out(c, 0), 2)], 15: [(lambda c: th_out(c, 1), 2)]}
            for n in list(STEPS) + [B + 2]:
                for h in range(H):
                    t = turning(n, h)
                    if t is not None:
                        probs(*t)
                    w = using(n, h)
                    if w is not None and w[1] % 2 == 1:
                        ctxA_out(w[0], w[1] // 2)
                    for f, back in table.get(h, []):
                        c = item(n, back)
                        if c is not None:
                            f(c)
            for b in range(B):
                if b == 0:
                    act.wait_ge(sm["hid_ready"], B)
                nc.scalar.activation(ghid[:, b, :], hid[:, b, :], ACT.Gelu).then_inc(sm["ghid_ready"], 1)
            for b in range(B):
                if b % 2 == 0:
                    act.wait_ge(sm["eo_done"], b // 2 + 1)
                nc.scalar.activation(eoT[0:A, b, :], EB[b // 2][0:A, (b % 2) * S:(b % 2 + 1) * S], ACT.Identity,
                                     bias=bsel[:, b:b + 1]).then_inc(sm["eo_ready"], 1)

        @block.vector
        def _(dve):
            def stats1(t0, t1):
                for t in range(t0, t1):
                    if t % QT == 0:
                        dve.wait_ge(x_in[t // QT], 16)
                    nc.vector.bn_stats(st1[:, t, :], x_sb[:, t // QT, t % QT, :]).then_inc(sm["stats1"], 1)
                for t in range(t0, t1):
                    dve.wait_ge(sm["stats1"], t0 + t + 1)
                    nc.vector.bn_aggr(mv1[:, t, :], st1[:, t, :]).then_inc(sm["stats1"], 1)

            stats1(0, QT)
            newton_seed(dve, mv1[:, 0:QT, 1], nt1[:, :, 0:QT], sm["stats1"], sm["y1_seed"], 2 * QT, 0, QT)
            nc.vector.memset(vaug[:, :, :, :, :], 0.0).then_inc(sm["ones_set"], 1)
            dve.wait_ge(sm["ones_set"], 1)
            nc.vector.memset(vaug[:, :, :, :, HD:HD + 1], 1.0).then_inc(sm["ones_set"], 1)

            dve.wait_ge(sm["t_in"], 16)
            dve.wait_ge(sm["cols_in"], 16)
            nc.vector.tensor_copy(emb[:, 0, :], emb_i[:, :]).then_inc(sm["emb_x"], 1)
            dve.wait_ge(sm["emb_x"], 1)
            nc.vector.tensor_scalar(emb[:, 1, :], emb[:, 0, :], RESCALE / STEPS_T, None, ALU.mult
                                    ).then_inc(sm["emb_x"], 1)
            dve.wait_ge(sm["emb_x"], 2)
            nc.vector.tensor_scalar(emb[:, 0, :], emb[:, 1, :], col(FREQ), None, ALU.mult
                                    ).then_inc(sm["emb_x"], 1)
            dve.wait_ge(sm["emb_x"], 3)
            chain = [0]

            def link(ins, s="emb_silu"):
                chain[0] += 1
                ins.then_inc(sm[s], 1)
                dve.wait_ge(sm[s], chain[0])

            link(nc.vector.tensor_scalar(emb[:, 1, :], emb[:, 0, :], 1.0 / 6.283185307179586, col(PHASE),
                                         ALU.mult, ALU.add))
            link(nc.vector.tensor_scalar(emb[:, 2, :], emb[:, 1, :], ROUND, ROUND, ALU.add, ALU.subtract))
            for tau in (TAU1, TAU2, TAU3):
                link(nc.vector.scalar_tensor_tensor(emb[:, 0, :], emb[:, 2, :], -tau, emb[:, 0, :],
                                                    ALU.mult, ALU.add))
            nc.vector.tensor_scalar(emb[:, 1, :], col(PHASE).to_broadcast([P, B]), 6.283185307179586, None,
                                    ALU.mult).then_inc(sm["emb_x"], 1)
            dve.wait_ge(sm["emb_x"], 4)
            nc.vector.tensor_tensor(out=emb[:, 5, :], in0=emb[:, 0, :], in1=emb[:, 1, :], op=ALU.add
                                    ).then_inc(sm["emb_x"], 1)
            dve.wait_ge(sm["emb_x"], 5)
            nc.vector.tensor_scalar(emb[:, 2, :], emb[:, 5, :], 3.1415925, -3.1415925, ALU.min, ALU.max
                                    ).then_inc(sm["emb_x"], 1)

            def norm1(b):
                if b >= 2:
                    dve.wait_ge(sm["t1_done"], b - 1)
                dve.wait_ge(sm["nt1_step"], NSTEP * (1 if b == 0 else 2))
                for t in range(QT):
                    k = b * QT + t
                    last = nc.vector.tensor_scalar(z1[:, b % 2, t, :], x_sb[:, b, t, :], mv1[:, k, 0:1],
                                                   nt1[:, 1, k:k + 1], ALU.subtract, ALU.mult)
                last.then_inc(sm["z1_ready"], 1)

            norm1(0)
            dve.wait_ge(sm["emb_exp"], 1)
            link(nc.vector.tensor_scalar(emb[:, 5, :], emb[:, 4, :], 1.0, None, ALU.add))
            link(nc.vector.reciprocal(emb[:, 6, :], emb[:, 5, :]))
            link(nc.vector.tensor_tensor(out=emb[:, 7, :], in0=emb[:, 3, :], in1=emb[:, 6, :], op=ALU.mult))
            dve.wait_ge(sm["ada_mm"], 1)
            nc.vector.tensor_scalar(ada[:, 0, :], MC[:, 0:B], col(BADA_S), 1.0, ALU.add, ALU.add
                                    ).then_inc(sm["ada_ready"], 1)
            nc.vector.tensor_scalar(ada[:, 1, :], MC[:, B:2 * B], col(BADA_H), None, ALU.add
                                    ).then_inc(sm["ada_ready"], 1)
            stats1(QT, B * QT)
            newton_seed(dve, mv1[:, QT:, 1], nt1[:, :, QT:], sm["stats1"], sm["y1_seed"],
                        2 * B * QT, NSEED, (B - 1) * QT)

            dve.wait_ge(sm["dom_in"], 16)
            dve.wait_ge(sm["w_in"], 16)
            E1 = A + 1
            dchain = [0]

            def dlink(ins):
                dchain[0] += 1
                ins.then_inc(sm["dom_ready"], 1)
                dve.wait_ge(sm["dom_ready"], dchain[0])

            dlink(nc.vector.tensor_copy(dom[:, 0, :], dom_i[:, :]))
            dlink(nc.vector.tensor_scalar(dom[:, 1, :], dom[:, 0, :], 0.0, float(NE - 1), ALU.max, ALU.min))
            dlink(nc.vector.tensor_tensor(out=dom[:, 2, :], in0=dom[:, 0, :], in1=dom[:, 1, :],
                                          op=ALU.is_equal))
            dlink(nc.vector.tensor_scalar(dom[:, 3, :], dom[:, 1, :], col(ECOL, 1, E1), None, ALU.is_equal))
            dlink(nc.vector.tensor_tensor(out=dom[:, 4, :], in0=dom[:, 3, :], in1=dom[:, 2, :], op=ALU.mult))
            dlink(nc.vector.tensor_scalar(dom[A:E1, 4, :], dom[A:E1, 2, :], -1.0, 1.0, ALU.mult, ALU.add))
            dlink(nc.vector.tensor_scalar(W2, W2, 0.5, None, ALU.mult))
            assert dchain[0] == 7
            dve.wait_ge(sm["wsel_mm"], 1)
            nc.vector.tensor_copy(wsel[:, :, :].rearrange("a b o -> a o b"),
                                  MC[0:A, 0:A * B].rearrange("a (o b) -> a o b", b=B)
                                  ).then_inc(sm["wsel_ready"], 1)
            nc.vector.tensor_copy(bsel[:, :], MC[0:A, A * B:A * B + B]).then_inc(sm["wsel_ready"], 1)

            def scores(n, k):
                g, t, pr = k // 4, k // 2 % 2, k % 2
                r = (n * NG + g) % RING
                dve.wait_ge(sm["scores_done"], H * n + k + 1)
                if t == 0 and pr == 0:
                    dve.wait_ge(f_in[r], 16 * ((n * NG + g) // RING + 1))
                if k == 0 and n >= 2:
                    dve.wait_ge(sm["nan_ready"], n - 1)
                    dve.wait_ge(sm["mrep_ready"], n - 1)
                for j in range(2):
                    hh = 2 * pr + j
                    last = nc.vector.tensor_tensor_reduce(
                        out=F[:, r, hh, t, :], in0=SB[k % 2][:, j * S:(j + 1) * S], in1=F[:, r, hh, t, :],
                        scale=1.0, scalar=-3.4e38, op0=ALU.add, op1=ALU.max,
                        accum_out=mx[:, n % 2, t, G * g + hh:G * g + hh + 1])
                last.then_inc(sm["scores_read"], 1)

            def v_out(b):
                dve.wait_ge(sm["vp_done"], b + 1)
                dve.wait_ge(sm["rows_in"], 16)
                dve.wait_ge(sm["ones_set"], 2)
                if b >= 2:
                    dve.wait_ge(sm["ctx_done"], NG * (b - 1))
                for t in range(QT):
                    last = nc.vector.tensor_tensor(
                        out=vaug[:, b % 2, t, :, 0:HD],
                        in0=MA[:, t * D:(t + 1) * D].rearrange("p (h d) -> p h d", h=H),
                        in1=rows_sb[:, 0, :].rearrange("p (h d) -> p h d", h=H), op=ALU.add)
                last.then_inc(sm["v_ready"], 1)

            def norm_ctx(c):
                dve.wait_ge(sm["tc_done"], 2 * (c + 1))
                dve.wait_ge(sm["nan_ready"], c + 1)
                if c >= 1:
                    dve.wait_ge(sm["tc2_done"], c)
                tb = [MB[:, :].rearrange("p (h e) -> p h e", h=H), MC[:, :].rearrange("p (h e) -> p h e", h=H)]
                for t in range(QT):
                    last = nc.vector.tensor_tensor(out=csum[:, t, :], in0=tb[t][:, :, HD],
                                                   in1=nanfix[:, c % 2, t, :], op=ALU.add)
                last.then_inc(sm["rsum_fixed"], 1)
                dve.wait_ge(sm["rsum_fixed"], c + 1)
                nc.vector.reciprocal(csum[:, :, :], csum[:, :, :]).then_inc(sm["rsum_inv"], 1)
                dve.wait_ge(sm["rsum_inv"], c + 1)
                for t in range(QT):
                    last = nc.vector.tensor_tensor(
                        out=ctxn[:, t, :].rearrange("p (h d) -> p h d", h=H), in0=tb[t][:, :, 0:HD],
                        in1=csum[:, t, :].unsqueeze(2).to_broadcast([P, H, HD]), op=ALU.mult)
                last.then_inc(sm["ctxn_ready"], 1)

            def stats2(c):
                dve.wait_ge(sm["x2_ready"], c + 1)
                if c >= 1:
                    dve.wait_ge(sm["z2_ready"], c)
                for t in range(QT):
                    nc.vector.bn_stats(st2[:, t, :], x2[:, c % 2, t, :]).then_inc(sm["stats2"], 1)
                for t in range(QT):
                    dve.wait_ge(sm["stats2"], 2 * QT * c + QT + t)
                    nc.vector.bn_aggr(mv2[:, c % 2, t, :], st2[:, t, :]).then_inc(sm["stats2"], 1)
                newton_seed(dve, mv2[:, c % 2, :, 1], nt2, sm["stats2"], sm["y2_seed"], 2 * QT * (c + 1),
                            NSEED * c, QT)

            def norm2(c):
                dve.wait_ge(sm["nt2_step"], NSTEP * (c + 1))
                if c >= 1:
                    dve.wait_ge(sm["t2_done"], c)
                for t in range(QT):
                    last = nc.vector.tensor_scalar(z2[:, t, :], x2[:, c % 2, t, :], mv2[:, c % 2, t, 0:1],
                                                   nt2[:, 1, t:t + 1], ALU.subtract, ALU.mult)
                last.then_inc(sm["z2_ready"], 1)

            def u_out(c, j):
                dve.wait_ge(sm["ff1_done"], 2 * c + j + 1)
                if c >= 1:
                    dve.wait_ge(sm["ff2_done"], c)
                nc.vector.tensor_tensor(out=u[:, 2 * j:2 * j + 2, :],
                                        in0=(MB, MC)[j][:, :].rearrange("p (f s) -> p f s", f=2),
                                        in1=col(B1 + 2 * j, 2).unsqueeze(2).to_broadcast([P, 2, S]),
                                        op=ALU.add).then_inc(sm["u_ready"], 1)

            def g_out(c, j):
                dve.wait_ge(sm["th_ready"], 2 * c + j + 1)
                uu = u[:, 2 * j:2 * j + 2, :]
                nc.vector.scalar_tensor_tensor(uu, th[:, 2 * j:2 * j + 2, :], 1.0, uu, ALU.add, ALU.mult
                                               ).then_inc(sm["g_ready"], 1)

            table = {0: [(lambda c: g_out(c, 0), 3), (lambda c: g_out(c, 1), 3)],
                     1: [(norm1, -1)], 8: [(norm_ctx, 2)], 9: [(v_out, 0)],
                     10: [(stats2, 2)], 12: [(norm2, 2)],
                     14: [(lambda c: u_out(c, 0), 2)], 15: [(lambda c: u_out(c, 1), 2)]}
            for n in list(STEPS) + [B + 2]:
                for h in range(H):
                    c = item(n, 0)
                    if c is not None:
                        scores(c, h)
                    for f, back in table.get(h, []):
                        c = item(n, back)
                        if c is not None and not (f is norm1 and c == 0):
                            f(c)

            for q in range(4):
                dve.wait_ge(sm["up_done"], q + 1)
                for t in range(4):
                    nc.vector.bn_stats(st3[:, 4 * q + t, :], UB[q][:, t * D:(t + 1) * D]
                                       ).then_inc(sm["st3_step"], 1)
                for t in range(4):
                    dve.wait_ge(sm["st3_step"], 8 * q + 4 + t)
                    nc.vector.bn_aggr(mv3[:, 4 * q + t, :], st3[:, 4 * q + t, :]).then_inc(sm["st3_step"], 1)
                nt = nt3[:, :, 4 * q:4 * q + 4]
                newton_seed(dve, mv3[:, 4 * q:4 * q + 4, 1], nt, sm["st3_step"], sm["y3_seed"], 8 * (q + 1),
                            NSEED * q, 4)
                newton_steps(nc.vector, nt, sm["y3_seed"], NSEED * (q + 1), sm["nt3_step"], NSTEP * q)
                dve.wait_ge(sm["nt3_step"], NSTEP * (q + 1))
                for t in range(4):
                    i = 4 * q + t
                    nc.vector.tensor_scalar(y[:, i // QT, i % QT, :], UB[q][:, t * D:(t + 1) * D],
                                            mv3[:, i, 0:1], nt3[:, 1, i:i + 1], ALU.subtract, ALU.mult
                                            ).then_inc(sm["norm3_ready"], 1)
                for t in range(4):
                    i = 4 * q + t
                    dve.wait_ge(sm["norm3_ready"], i + 1)
                    nc.vector.tensor_tensor(out=y[:, i // QT, i % QT, :], in0=y[:, i // QT, i % QT, :],
                                            in1=rows_sb[:, 1, :], op=ALU.mult).then_inc(sm["z3_ready"], 1)

        @block.tensor
        def _(pe):
            mm = nc.tensor.matmul

            def turn(dst, src, start=True, stop=True):
                return mm(dst, src, idf[:, :], start=start, stop=stop, is_transpose=True)

            def turn_z1(b):
                pe.wait_ge(sm["z1_ready"], b + 1)
                if b == 0:
                    pe.wait_ge(sm["idf_in"], 16)
                if b >= 2:
                    pe.wait_ge(sm["v_ready"], b - 1)
                if b >= 2:
                    pe.wait_ge(sm["mT_ready"], b - 1)
                for t in range(QT):
                    last = turn(MA[:, t * P:(t + 1) * P], z1[:, b % 2, t, :])
                last.then_inc(sm["t1_done"], 1)

            def project_qk(b):
                pe.wait_ge(sm["x1T_ready"], b + 1)
                mm(MA[:, 0:S], WQ, x1T[:, b, :], start=True, stop=True)
                mm(MA[:, S:2 * S], WK, x1T[:, b, :], start=True, stop=True).then_inc(sm["qkp_done"], 1)

            def project_v(b):
                pe.wait_ge(sm["qk_ready"], 2 * min(b + 2, B))
                for t in range(QT):
                    last = mm(MA[:, t * D:(t + 1) * D], x1T[:, b, t * P:(t + 1) * P], WV, start=True, stop=True)
                last.then_inc(sm["vp_done"], 1)

            def turn_max(c):
                pe.wait_ge(sm["mrep_ready"], c + 1)
                pe.wait_ge(sm["v_ready"], c + 1)
                for t in range(QT):
                    last = turn(MA[0:96, t * P:(t + 1) * P],
                                mrep[:, c % 2, t, :, :].rearrange("p i h -> p (i h)"))
                last.then_inc(sm["tm_done"], 1)

            def score(n, k):
                g, t, pr = k // 4, k // 2 % 2, k % 2
                bank = SB[k % 2]
                if k == 0:
                    pe.wait_ge(sm["maskb_ready"], n + 1)
                    pe.wait_ge(q_in[n % 2], 16 * (n // 2 + 1))
                    pe.wait_ge(k_in[n % 2], 16 * NPARTS * (n // 2 + 1))
                    if n == 0:
                        pe.wait_ge(sm["idb_in"], 16)
                if H * n + k >= 2:
                    pe.wait_ge(sm["scores_read"], H * n + k - 1)
                mm(bank[:, :].rearrange("p (j s) -> p j s", j=2), idb[:, :],
                   maskb[:, n % 2, t:t + 1, :].to_broadcast([P, 2, S]), start=True, stop=False)
                for j in range(2):
                    h = G * g + 2 * pr + j
                    last = mm(bank[:, j * S:(j + 1) * S], qstack[:, n % 2, h, t * P:(t + 1) * P],
                              kstack[:, n % 2, h, :], start=False, stop=(j == 1))
                last.then_inc(sm["scores_done"], 1)

            def turn_scores(c, h):
                k = H * c + h
                bank = ZB[k % 2]
                if h == 0:
                    pe.wait_ge(sm["msplit_step"], 4 * (c + 1))
                    pe.wait_ge(sm["scores_read"], H * (c + 1))
                    if c == 0:
                        pe.wait_ge(sm["sel_in"], 16)
                if k >= 2:
                    pe.wait_ge(sm["probs_ready"], k - 1)
                r = (c * NG + h // G) % RING
                for kt in range(QT):
                    for t in range(QT):
                        turn(bank[:, kt * S + t * P:kt * S + (t + 1) * P],
                             F[:, r, h % G, t, kt * P:(kt + 1) * P],
                             start=(kt == 0 and t == 0), stop=False)
                mm(bank[:, :].rearrange("p (j s) -> p j s", j=QT), negsel_sb[:, h, :],
                   mstack[:, c % 2, :].unsqueeze(1).to_broadcast([96, QT, S]),
                   start=False, stop=True).then_inc(sm["turned"], 1)

            def context(c, g):
                pe.wait_ge(sm["probs_ready"], H * c + G * (g + 1))
                if g == 0:
                    pe.wait_ge(sm["v_ready"], c + 1)
                if g % 2 == 0 and NG * c + g >= 2:
                    pe.wait_ge(sm["ctxA_ready"], (NG * c + g) // 2)
                for kt in range(QT):
                    for j in range(G):
                        h = G * g + j
                        last = mm(CB[32 * j:32 * j + 32, (g % 2) * S:(g % 2 + 1) * S],
                                  vaug[:, c % 2, kt, h, :], PT[:, (H * c + h) % NPT, kt, :],
                                  start=(kt == 0), stop=(kt == QT - 1))
                last.then_inc(sm["ctx_done"], 1)

            def turn_ctx(c):
                pe.wait_ge(sm["ctxA_ready"], 2 * (c + 1))
                if c == 0:
                    pe.wait_ge(sm["wsel_ready"], 2)
                else:
                    pe.wait_ge(sm["x3_ready"], c)
                    pe.wait_ge(sm["hid_ready"], c)
                for t in range(QT):
                    for g in range(NG):
                        last = turn((MB, MC)[t][:, g * P:(g + 1) * P], ctxA[:, g, t * P:(t + 1) * P])
                    last.then_inc(sm["tc_done"], 1)

            def turn_ctxn(c):
                pe.wait_ge(sm["ctxn_ready"], c + 1)
                for t in range(QT):
                    last = turn(MB[:, t * P:(t + 1) * P], ctxn[:, t, :])
                last.then_inc(sm["tc2_done"], 1)

            def out_project(c):
                pe.wait_ge(sm["ctxT_ready"], c + 1)
                if c == 0:
                    pe.wait_ge(sm["bo_in"], 16)
                    pe.wait_ge(sm["pads_set"], 1)
                for t in range(QT):
                    o = MC[:, t * D:(t + 1) * D]
                    mm(o, ctxT[:, t * P:(t + 1) * P], WO, start=True, stop=False)
                    mm(o, ones_row[:, :], bo_sb[:, :], start=False, stop=False)
                    last = turn(o, x1T[:, c, t * P:(t + 1) * P], start=False, stop=True)
                last.then_inc(sm["o_done"], 1)

            def turn_z2(c):
                pe.wait_ge(sm["z2_ready"], c + 1)
                for t in range(QT):
                    last = turn(MB[:, S + t * P:S + (t + 1) * P], z2[:, t, :])
                last.then_inc(sm["t2_done"], 1)

            def ff1(c, j):
                if j == 0:
                    pe.wait_ge(sm["hT_ready"], c + 1)
                else:
                    pe.wait_ge(sm["x2_ready"], c + 1)
                for i in range(2):
                    f = 2 * j + i
                    last = mm((MB, MC)[j][:, i * S:(i + 1) * S], W1[:, f * P:(f + 1) * P], hT[:, :],
                              start=True, stop=True)
                last.then_inc(sm["ff1_done"], 1)

            def ff2(c):
                pe.wait_ge(sm["g_ready"], 2 * (c + 1))
                for f in range(FF):
                    mm(MB[:, 0:S], W2[:, f * P:(f + 1) * P], u[:, f, :], start=(f == 0), stop=False)
                for t in range(QT):
                    last = turn(MB[:, t * P:(t + 1) * P], x2[:, c % 2, t, :], start=False, stop=(t == QT - 1))
                last.then_inc(sm["ff2_done"], 1)

            def down_project(c):
                pe.wait_ge(sm["x3_ready"], c + 1)
                if c == 0:
                    pe.wait_ge(sm["down_in"], 16)
                mm(MC[0:A, 0:S], down_sb[:, :], x3T[:, c, :], start=True, stop=True).then_inc(sm["dn_done"], 1)

            pe.wait_ge(sm["w_in"], 16)
            pe.wait_ge(sm["emb_silu"], 8)
            mm(MC[:, 0:B], WADA[:, 0:D], emb[:, 7, :], start=True, stop=True)
            mm(MC[:, B:2 * B], WADA[:, D:2 * D], emb[:, 7, :], start=True, stop=True).then_inc(sm["ada_mm"], 1)
            turn_z1(0)
            project_qk(0)
            pe.wait_ge(sm["expert_in"], 16)
            pe.wait_ge(sm["dom_ready"], 7)
            pe.wait_ge(sm["ada_ready"], 2)
            for o in range(A):
                mm(MC[0:A, o * B:(o + 1) * B], expert_sb[:, o * A:(o + 1) * A], dom[:, 4, :],
                   start=True, stop=True)
            mm(MC[0:A, A * B:A * B + B], expert_sb[:, A * A:A * A + A], dom[:, 4, :], start=True, stop=False)
            mm(MC[0:A, A * B:A * B + B], expert_sb[:, A * A + A:A * A + 2 * A], dom[:, 3, :],
               start=False, stop=True).then_inc(sm["wsel_mm"], 1)

            table = {0: [(ff2, 3)], 1: [(turn_max, 1)], 2: [(turn_z1, -1), (down_project, 3)],
                     4: [(project_qk, -1)], 7: [(turn_ctx, 2)], 8: [(project_v, 0)], 9: [(turn_ctxn, 2)],
                     10: [(out_project, 2)], 12: [(turn_z2, 2)],
                     14: [(lambda c: ff1(c, 0), 2)], 15: [(lambda c: ff1(c, 1), 2)]}
            for n in list(STEPS) + [B + 2]:
                for h in range(H):
                    c = item(n, 0)
                    if c is not None:
                        score(c, h)
                    t = turning(n, h)
                    if t is not None:
                        turn_scores(*t)
                    w = using(n, h)
                    if w is not None:
                        context(*w)
                    for f, back in table.get(h, []):
                        c = item(n, back)
                        if c is not None and not (f in (turn_z1, project_qk) and c == 0):
                            f(c)

            pe.wait_ge(sm["up_in"], 16)
            pe.wait_ge(sm["pads_set"], 2)
            pe.wait_ge(sm["probs_ready"], H * B)
            pe.wait_ge(sm["ctxA_ready"], 2 * B)
            for b in range(B):
                pe.wait_ge(sm["ghid_ready"], b + 1)
                last = mm(EB[b // 2][0:A, (b % 2) * S:(b % 2 + 1) * S], wsel[:, b, :], ghid[:, b, :],
                          start=True, stop=True)
                if b % 2 == 1:
                    last.then_inc(sm["eo_done"], 1)
            for b in range(B):
                pe.wait_ge(sm["eo_ready"], b + 1)
                for t in range(QT):
                    i = b * QT + t
                    o = UB[i // 4][:, (i % 4) * D:(i % 4 + 1) * D]
                    mm(o, eoT[:, b, t * P:(t + 1) * P], up_sb[:, :], start=True, stop=False)
                    last = turn(o, x3T[:, b, t * P:(t + 1) * P], start=False, stop=True)
                if b % 2 == 1:
                    last.then_inc(sm["up_done"], 1)


def kernel(**inputs):
    import math
    import ml_dtypes
    import numpy as np
    import concourse.bacc as bacc
    from concourse import mybir
    from concourse.bass_utils import run_bass_kernel_spmd

    a = {k: np.asarray(v) for k, v in inputs.items()}
    f32 = np.float32
    B, S, D = a["x"].shape
    H = a["fside_Bx16xSxS_0"].shape[1]
    A = a["L1_cond_down_W"].shape[0]
    NE = a["L1_cond_expert_W"].shape[0]
    P, half = 128, D // 2
    freqs = np.exp(np.arange(half, dtype=f32) * f32(-math.log(10000.0) / (half - 1))).astype(f32)
    freq = np.concatenate([freqs, freqs])
    phase = np.concatenate([np.zeros(half, f32), np.full(half, 0.25, f32)])
    ecol = np.full(P, -1.0, f32)
    ecol[:NE] = np.arange(NE)
    negsel = np.zeros((96, H, P), ml_dtypes.bfloat16)
    for i in range(3):
        for h in range(H):
            negsel[32 * i + h, h, :] = -1.0
    L0 = lambda n: a["L0_cond_" + n]
    L1 = lambda n: a["L1_cond_" + n]
    w2 = L0("W2").reshape(4, P, D).transpose(1, 0, 2).reshape(P, 4 * D)
    wts = np.concatenate([L0("Wq"), L0("Wk"), L0("Wv"), L0("Wo"), L0("W_ada"), L0("W1"), w2], axis=1)
    downb = np.zeros(P, f32)
    downb[:A] = L1("down_b")
    cols = np.stack([L0("b_ada")[:D], L0("b_ada")[D:], L0("bq"), L0("bk"), L0("g2"), L0("beta2"), L0("b2"),
                     freq, phase, ecol, downb, *L0("b1").reshape(4, P)], axis=1)
    rows = np.stack([L0("bv"), L1("ln_gamma"), L1("ln_beta")])
    expert = np.zeros((A + 1, A * A + 2 * A), f32)
    expert[:NE, :A * A] = L1("expert_W").reshape(NE, A * A)
    expert[A, :A * A] = np.eye(A, dtype=f32).reshape(-1)
    expert[:NE, A * A:A * A + A] = L1("expert_b")
    expert[:NE, A * A + A:] = L1("domain_emb")
    up = np.concatenate([L1("up_W").T, L1("up_b")[None, :]], axis=0)
    arrays = {
        "x": a["x"], "tstep": a["itok_B_34_63"], "fside": a["fside_Bx16xSxS_0"], "domain": a["itok_B_0_15"],
        "mask": a["mask_Bx1xSxS_bk0"], "wts": wts, "cols": cols, "rows": rows,
        "bo": L0("bo")[None, :], "down": L1("down_W").T, "up": up, "expert": expert,
        "identf": np.eye(P, dtype=f32), "identb": np.eye(P, dtype=f32).astype(ml_dtypes.bfloat16),
        "negsel": negsel,
    }
    nc = bacc.Bacc("TRN2", target_bir_lowering=False, num_devices=1)
    named, args = {}, []
    for name, v in arrays.items():
        v = np.ascontiguousarray(v)
        named[f"in_{name}"] = v
        args.append(nc.dram_tensor(f"in_{name}", v.shape, mybir.dt.from_np(v.dtype), kind="ExternalInput").ap())
    args.append(nc.dram_tensor("out_0", (B, S, D), mybir.dt.float32, kind="ExternalOutput").ap())
    cond_seq_kernel(nc, *args)
    r = run_bass_kernel_spmd(nc, [named], core_ids=[0])
    return r.results[0]["out_0"]
```

```python
import concourse.bass as bass
from concourse import mybir
from contextlib import ExitStack


def cond_seq_kernel(nc, x, tstep, fside, domain, mask, wts, cols, rows, bo, down, up, expert,
                    identf, identb, out):
    fp32 = mybir.dt.float32
    bf16 = mybir.dt.bfloat16
    i32 = mybir.dt.int32
    u8 = mybir.dt.uint8
    ALU = mybir.AluOpType
    ACT = mybir.ActivationFunctionType

    B, S, D = x.shape
    H = fside.shape[1]
    HD = D // H
    P = 128
    QT = S // P
    FF = 4
    A = down.shape[1]
    NE = 16
    G = 4
    NG = H // G
    QS = float(HD) ** -0.5
    EPS = 1e-5
    MASKED = -3.0e38
    RING = 8
    NPT = 8
    NPARTS = 3
    KROWS = NPARTS * NPARTS * HD
    LAG = 4
    TAU1 = 6.28125
    TAU2 = 0.0019350051879882812
    TAU3 = 6.283185307179586 - TAU1 - TAU2
    RESCALE, STEPS_T = 4000.0, 100.0
    ROUND = 12582912.0
    ROUNDS = 3
    MAGIC = float(0x5F3759DF)

    parts_dram = nc.dram_tensor("parts_dram", [2, 2, HD, NPARTS, H, S], bf16).ap()

    ctx = ExitStack()
    with ctx:
        def sb(name, shape, dt=fp32):
            return ctx.enter_context(nc.sbuf_tensor(name, shape, dt))

        def sem(name):
            return ctx.enter_context(nc.semaphore(name))

        wts_sb = sb("wts_sb", [P, wts.shape[1]])
        WQ, WK, WV, WO = (wts_sb[:, i * D:(i + 1) * D] for i in range(4))
        WADA = wts_sb[:, 4 * D:6 * D]
        W1 = wts_sb[:, 6 * D:6 * D + FF * P]
        W2 = wts_sb[:, 6 * D + FF * P:6 * D + 2 * FF * P]
        cols_sb = sb("cols_sb", [P, cols.shape[1]])
        (BADA_S, BADA_H, BQ, BK, G2, BETA2, B2, FREQ, PHASE, ECOL, DOWNB) = range(11)
        B1 = 11

        def col(i, n=1, p=P):
            return cols_sb[0:p, i:i + n]

        rows_sb = sb("rows_sb", [P, 3, D])
        bo_sb = sb("bo_sb", [1, D])
        down_sb = sb("down_sb", [P, A])
        up_sb = sb("up_sb", [A + 1, D])
        idf = sb("idf", [P, P])
        idb = sb("idb", [P, P], bf16)
        ones_row = sb("ones_row", [1, P])

        x_sb = sb("x_sb", [P, B, QT, D])
        st1 = sb("st1", [P, B * QT, 6])
        mv1 = sb("mv1", [P, B * QT, 2])
        nt1 = sb("nt1", [P, 4, B * QT])
        z1 = sb("z1", [P, 2, QT, D])
        x1T = sb("x1T", [P, B, S])
        qkf = sb("qkf", [P, 2, S])
        parts = sb("parts", [P, 2, NPARTS, S], bf16)
        qk_rest = sb("qk_rest", [P, 2, S])
        qstack = sb("qstack", [P, 2, H, S], bf16)
        kstack = sb("kstack", [P, 2, H, S], bf16)
        vaug = sb("vaug", [P, 2, QT, H, 32])
        mask_sb = sb("mask_sb", [P, 2, QT, S], u8)
        maskb = sb("maskb", [P, 2, QT, S], bf16)
        F = sb("F", [P, RING, G, QT, S])
        mx = sb("mx", [P, 2, QT, H])
        nanfix = sb("nanfix", [P, 2, QT, H])
        PT = sb("PT", [P, NPT, QT, S])
        ctxA = sb("ctxA", [P, NG, S])
        csum = sb("csum", [P, QT, H])
        ctxn = sb("ctxn", [P, QT, D])
        ctxT = sb("ctxT", [P, S])
        x2 = sb("x2", [P, 2, QT, D])
        st2 = sb("st2", [P, QT, 6])
        mv2 = sb("mv2", [P, 2, QT, 2])
        nt2 = sb("nt2", [P, 4, QT])
        z2 = sb("z2", [P, QT, D])
        hT = sb("hT", [P, S])
        u = sb("u", [P, FF, S])
        th = sb("th", [P, FF, S])
        x3T = sb("x3T", [P, B, S])
        hid = sb("hid", [A, B, S])
        ghid = hid
        expert_sb = PT[0:A + 1, :, :, :].rearrange("p n t s -> p (n t s)")[:, 0:expert.shape[1]]
        eoT = PT[0:A + 1, 0:4, :, :].rearrange("p n t s -> p (n t) s")
        emb = sb("emb", [P, 8, B])
        emb_i = sb("emb_i", [P, B], i32)
        dom_i = sb("dom_i", [A + 1, B], i32)
        dom = sb("dom", [A + 1, 6, B])
        ada = sb("ada", [P, 2, B])
        qbias = sb("qbias", [P, 1])
        wsel = sb("wsel", [A, B, A])
        bsel = sb("bsel", [A, B])
        st3 = sb("st3", [P, B * QT, 6])
        mv3 = sb("mv3", [P, B * QT, 2])
        nt3 = sb("nt3", [P, 4, B * QT])
        y = x_sb

        banks = [ctx.enter_context(nc.psum_tensor(f"bank{i}", [P, 512], fp32)) for i in range(8)]
        SB = banks[0:2]
        ZB = banks[2:4]
        CB = banks[4]
        MA, MB, MC = banks[5:8]

        EB = [ZB[0], CB, ZB[0], ZB[0]]
        UB = [SB[0], SB[1], ZB[1], CB]

        names = """w_in w2_in w2_halved cols_in rows_in bo_in down_in up_in expert_in idf_in idb_in
            t_in dom_in ones_set pads_set stack_pads_set
            emb_x emb_sin emb_exp emb_silu ada_mm ada_ready dom_ready wsel_mm wsel_ready
            stats1 y1_seed nt1_step z1_ready t1_done x1T_ready qkp_done qk_ready rest_ready part2_ready parts_ready
            vp_done v_ready maskb_ready scores_done scores_read even_centered odd_centered
            nan_ready turned probs_ready ctx_done ctxA_ready tc_done rsum_fixed rsum_inv
            ctxn_ready tc2_done ctxT_ready o_done x2_ready stats2 y2_seed nt2_step z2_ready
            t2_done hT_ready ff1_done u_ready th_ready g_ready ff2_done x3_ready dn_done hid_ready
            ghid_ready eo_done eo_ready up_done st3_step y3_seed nt3_step norm3_ready y_step y_ready
            out_done""".split()
        sm = {n: sem(n) for n in names}
        x_in = [sem(f"x_in{i}") for i in range(B)]
        mask_in = [sem(f"mask_in{i}") for i in range(2)]
        f_in = [sem(f"f_in{i}") for i in range(RING)]
        q_in = [sem(f"q_in{i}") for i in range(2)]
        k_in = [sem(f"k_in{i}") for i in range(2)]

        parts_out = [sem(f"parts_out{i}") for i in range(2)]

        block = ctx.enter_context(nc.Block())
        STEPS = range(-1, B + 2)
        NPAIR = B // 2

        def pair(n, j):
            return n == B + (j == NPAIR - 1)

        def item(n, back):
            return n - back if 0 <= n - back < B else None

        def turning(n, h):
            s = H * n + h - LAG
            return (s // H, s % H) if 0 <= s < B * H else None

        def using(n, h):
            s = H * n + h - LAG - (G - 1) - 2
            return (s // H, s % H // G) if 0 <= s < B * H and s % G == 0 else None

        def newton_seed(dve, mv, nt, stats_sem, seed_sem, v0, s0, n):
            dve.wait_ge(stats_sem, v0)
            nc.vector.tensor_scalar(nt[:, 2, :], mv, EPS, None, ALU.add).then_inc(seed_sem, 1)
            dve.wait_ge(seed_sem, s0 + 1)
            nc.vector.tensor_scalar(nt[:, 0, :], nt[:, 2, :], -0.5, None, ALU.mult).then_inc(seed_sem, 1)
            nc.vector.tensor_scalar(nt[:, 3, :].bitcast(i32), nt[:, 2, :].bitcast(i32), 1, None,
                                    ALU.logical_shift_right).then_inc(seed_sem, 1)
            dve.wait_ge(seed_sem, s0 + 3)
            nc.vector.tensor_scalar(nt[:, 1, :].bitcast(i32), nt[:, 3, :].bitcast(i32), -1.0, MAGIC,
                                    ALU.mult, ALU.add).then_inc(seed_sem, 1)

        def newton_round(dve, nt, step_sem, k):
            if k:
                dve.wait_ge(step_sem, 3 * k)
            nc.vector.tensor_tensor(out=nt[:, 2, :], in0=nt[:, 1, :], in1=nt[:, 1, :],
                                    op=ALU.mult).then_inc(step_sem, 1)
            dve.wait_ge(step_sem, 3 * k + 1)
            nc.vector.tensor_tensor(out=nt[:, 3, :], in0=nt[:, 2, :], in1=nt[:, 0, :],
                                    op=ALU.mult).then_inc(step_sem, 1)
            dve.wait_ge(step_sem, 3 * k + 2)
            nc.vector.scalar_tensor_tensor(nt[:, 1, :], nt[:, 3, :], 1.5, nt[:, 1, :],
                                           ALU.add, ALU.mult).then_inc(step_sem, 1)

        def newton_steps(dve, nt, seed_sem, s0, step_sem, k0):
            dve.wait_ge(seed_sem, s0)
            for r in range(ROUNDS):
                newton_round(dve, nt, step_sem, k0 + r)

        NSTEP = 3 * ROUNDS
        NSEED = 4

        @block.sync
        def _(sp):
            def load_x(b):
                sp.dma_start(x_sb[:, b, :, :], x[b].rearrange("(t p) d -> p t d", p=P)).then_inc(x_in[b], 16)

            def load_mask(b):
                if b >= 2:
                    sp.wait_ge(sm["maskb_ready"], b - 1)
                sp.dma_start(mask_sb[:, b % 2, :, :],
                             mask[b, 0].rearrange("(t p) k -> p t k", p=P)).then_inc(mask_in[b % 2], 16)

            def load_bias(b, g):
                r = (b * NG + g) % RING
                if b >= 2:
                    sp.wait_ge(sm["turned"], H * (b - 2) + G * (g + 1))
                sp.dma_start(F[:, r, :, :, :],
                             fside[b, G * g:G * (g + 1)].rearrange("h (t p) k -> p h t k", p=P)
                             ).then_inc(f_in[r], 16)

            sp.dma_start(emb_i[:, :], tstep.rearrange("(o b) -> o b", o=1).to_broadcast([P, B])
                         ).then_inc(sm["t_in"], 16)
            sp.dma_start(cols_sb[:, :], cols).then_inc(sm["cols_in"], 16)
            load_x(0)
            sp.dma_start(wts_sb[:, :6 * D], wts[:, :6 * D]).then_inc(sm["w_in"], 16)
            sp.dma_start(idf[:, :], identf).then_inc(sm["idf_in"], 16)
            load_mask(0)
            sp.dma_start(idb[:, :], identb).then_inc(sm["idb_in"], 16)
            load_bias(0, 0)
            for b in range(1, B):
                load_x(b)
            sp.dma_start(rows_sb[:, :, :], rows.rearrange("(o r) d -> o r d", o=1).to_broadcast([P, 3, D])
                         ).then_inc(sm["rows_in"], 16)
            sp.dma_start(dom_i[:, :], domain.rearrange("(o b) -> o b", o=1).to_broadcast([A + 1, B])
                         ).then_inc(sm["dom_in"], 16)
            sp.dma_start(expert_sb, expert).then_inc(sm["expert_in"], 16)

            for b in range(B):
                if b >= 1:
                    load_mask(b)
                    load_bias(b, 0)
                else:
                    sp.wait_ge(sm["stack_pads_set"], 1)
                for w in range(2):
                    for i in range(NPARTS):
                        if i == 0:
                            sp.wait_ge(sm["qk_ready"], 4 * b + 2 * (w + 1))
                        else:
                            sp.wait_ge((sm["part2_ready"], sm["parts_ready"])[i - 1],
                                       (b + 1, 2 * b + w + 1)[i - 1])
                        sp.dma_start(parts_dram[b % 2, w, :, i].rearrange("d h s -> h d s"),
                                     parts[:, w, i, :]).then_inc(parts_out[w], 16)
                if b >= 2:
                    sp.wait_ge(sm["scores_done"], H * (b - 1))
                pq = parts_dram[b % 2, 0].rearrange("d i h s -> (d i) (h s)")
                pk = parts_dram[b % 2, 1].rearrange("d j h s -> j d (h s)")
                sp.wait_ge(parts_out[0], 16 * NPARTS * (b + 1))
                sp.dma_start(qstack[0:KROWS, b % 2, :, :].rearrange("p h s -> p (h s)"),
                             pq.unsqueeze(1).to_broadcast([HD * NPARTS, NPARTS, H * S])
                             ).then_inc(q_in[b % 2], 16)
                sp.wait_ge(parts_out[1], 16 * NPARTS * (b + 1))
                for j in range(NPARTS):
                    sp.dma_start(kstack[j:KROWS:NPARTS, b % 2, :, :].rearrange("p h s -> p (h s)"),
                                 pk[j].unsqueeze(1).to_broadcast([HD, NPARTS, H * S])
                                 ).then_inc(k_in[b % 2], 16)
                for g in range(1, NG):
                    load_bias(b, g)
                if b == 0:
                    sp.dma_start(wts_sb[:, 6 * D:], wts[:, 6 * D:]).then_inc(sm["w2_in"], 16)
                    sp.dma_start(bo_sb[:, :], bo).then_inc(sm["bo_in"], 16)
                    sp.dma_start(down_sb[:, :], down).then_inc(sm["down_in"], 16)
                    sp.dma_start(up_sb[:, :], up).then_inc(sm["up_in"], 16)

            for b in range(B):
                sp.wait_ge(sm["y_ready"], QT * (b + 1))
                sp.dma_start(out[b].rearrange("(t p) d -> p t d", p=P), y[:, b, :, :]).then_inc(sm["out_done"], 16)
            sp.wait_ge(sm["out_done"], 16 * B)

        @block.gpsimd
        def _(pool):
            pool.memset(ones_row[:, :], 1.0).then_inc(sm["pads_set"], 1)
            pool.wait_ge(sm["pads_set"], 1)
            for st in (qstack, kstack):
                last = pool.memset(st[64:P, :, :, :].rearrange("p n h s -> p (n h s)").bitcast(i32), 0)
            last.then_inc(sm["stack_pads_set"], 1)
            pool.wait_ge(sm["stack_pads_set"], 1)

            def center(n, h):
                r = (n * NG + h // G) % RING
                pool.wait_ge(sm["scores_read"], H * n + h + 1)
                z = F[:, r, h % G, :, :]
                pool.tensor_tensor(out=z, in0=z, in1=mx[:, n % 2, :, h:h + 1].to_broadcast([P, QT, S]),
                                   op=ALU.subtract).then_inc(sm["odd_centered"], 1)

            def nan_fix(n):
                if n >= 2:
                    pool.wait_ge(sm["rsum_fixed"], n - 1)
                pool.tensor_scalar(nanfix[:, n % 2, :, :], mx[:, n % 2, :, :], 2.0, 0.0,
                                   ALU.mult, ALU.mult).then_inc(sm["nan_ready"], 1)

            def qk_rest_out(b):
                pool.wait_ge(sm["qk_ready"], 4 * (b + 1))
                if b >= 1:
                    pool.wait_ge(sm["part2_ready"], b)
                pool.tensor_tensor(out=qk_rest[:, :, :], in0=qkf[:, :, :], in1=parts[:, :, 0, :],
                                   op=ALU.subtract).then_inc(sm["rest_ready"], 1)

            def qk_part3(b, w):
                pool.wait_ge(sm["part2_ready"], b + 1)
                pool.tensor_tensor(out=parts[:, w, 2, :], in0=qk_rest[:, w, :], in1=parts[:, w, 1, :],
                                   op=ALU.subtract).then_inc(sm["parts_ready"], 1)

            def eo_ones(n):
                pool.wait_ge(sm["ctx_done"], NG * B)
                pool.wait_ge(sm["nan_ready"], B)
                pool.memset(eoT[A:A + 1, :, :], 1.0).then_inc(sm["pads_set"], 1)
                pool.wait_ge(sm["pads_set"], 2)

            def gamma_beta(q):
                for t in range(4):
                    i = 4 * q + t
                    yt = y[:, i // QT, i % QT, :]
                    pool.wait_ge(sm["norm3_ready"], i + 1)
                    pool.tensor_tensor(out=yt, in0=yt, in1=rows_sb[:, 1, :], op=ALU.mult
                                       ).then_inc(sm["y_step"], 1)
                    pool.wait_ge(sm["y_step"], i + 1)
                    pool.tensor_tensor(out=yt, in0=yt, in1=rows_sb[:, 2, :], op=ALU.add
                                       ).then_inc(sm["y_ready"], 1)

            table = {5: [(qk_rest_out, -1)], 7: [(lambda b: qk_part3(b, 0), -1)],
                     8: [(lambda b: qk_part3(b, 1), -1)], 15: [(nan_fix, 0)]}
            for n in STEPS:
                for h in range(H):
                    c = item(n, 0)
                    if c is not None and h % 2 == 1:
                        center(c, h)
                    for f, back in table.get(h, []):
                        c = item(n, back)
                        if c is not None:
                            f(c)
                if n == B:
                    eo_ones(n)
                for q in range(NPAIR):
                    if pair(n, q):
                        gamma_beta(q)

        @block.scalar
        def _(act):
            act.wait_ge(sm["emb_x"], 6)
            nc.scalar.activation(emb[:, 3, :], emb[:, 2, :], ACT.Sin).then_inc(sm["emb_sin"], 1)
            act.wait_ge(sm["emb_sin"], 1)
            nc.scalar.activation(emb[:, 4, :], emb[:, 3, :], ACT.Exp, scale=-1.0).then_inc(sm["emb_exp"], 1)
            act.wait_ge(sm["cols_in"], 16)
            nc.scalar.activation(qbias[:, :], col(BQ), ACT.Copy, scale=QS)

            def x1T_out(b):
                act.wait_ge(sm["t1_done"], b + 1)
                act.wait_ge(sm["ada_ready"], 2)
                nc.scalar.activation(x1T[:, b, :], MA[:, 0:S], ACT.Identity, bias=ada[:, 1, b:b + 1],
                                     scale=ada[:, 0, b:b + 1]).then_inc(sm["x1T_ready"], 1)

            def mask_bias(b):
                act.wait_ge(mask_in[b % 2], 16 * (b // 2 + 1))
                if b >= 2:
                    act.wait_ge(sm["scores_done"], H * (b - 1))
                nc.scalar.activation(maskb[:, b % 2, :, :], mask_sb[:, b % 2, :, :], ACT.Copy,
                                     scale=MASKED).then_inc(sm["maskb_ready"], 1)

            def qk_out(b):
                act.wait_ge(sm["qkp_done"], b + 1)
                if b >= 1:
                    act.wait_ge(sm["rest_ready"], b)
                    for w in range(2):
                        act.wait_ge(parts_out[w], 16 * NPARTS * b)
                for w, bias, scale in ((0, qbias[:, :], QS), (1, col(BK), 1.0)):
                    for dst in (qkf[:, w, :], parts[:, w, 0, :]):
                        nc.scalar.activation(dst, MA[:, w * S:(w + 1) * S], ACT.Identity, bias=bias, scale=scale
                                             ).then_inc(sm["qk_ready"], 1)

            def probs(c, h):
                k = H * c + h
                act.wait_ge(sm["turned"], k + 1)
                if k == 0:
                    act.wait_ge(sm["wsel_mm"], 1)
                if k >= NPT:
                    act.wait_ge(sm["ctx_done"], (k - NPT) // G + 1)
                nc.scalar.activation(PT[:, k % NPT, :, :], ZB[k % 2][:, :].rearrange("p (t q) -> p t q", t=QT),
                                     ACT.Exp).then_inc(sm["probs_ready"], 1)

            def ctxA_out(c, j):
                act.wait_ge(sm["ctx_done"], NG * c + 2 * (j + 1))
                if c >= 1:
                    act.wait_ge(sm["tc_done"], 2 * c)
                nc.scalar.activation(ctxA[:, 2 * j:2 * j + 2, :],
                                     CB[:, :].rearrange("p (g q) -> p g q", g=2), ACT.Copy
                                     ).then_inc(sm["ctxA_ready"], 1)

            def ctxT_out(c):
                act.wait_ge(sm["tc2_done"], c + 1)
                if c >= 1:
                    act.wait_ge(sm["o_done"], c)
                nc.scalar.activation(ctxT[:, :], MB[:, 0:S], ACT.Copy).then_inc(sm["ctxT_ready"], 1)

            def x2_out(c):
                act.wait_ge(sm["o_done"], c + 1)
                if c >= 2:
                    act.wait_ge(sm["ff2_done"], c - 1)
                nc.scalar.activation(x2[:, c % 2, :, :], MC[:, 0:S].rearrange("p (t d) -> p t d", t=QT),
                                     ACT.Copy).then_inc(sm["x2_ready"], 1)

            def hT_out(c):
                act.wait_ge(sm["t2_done"], c + 1)
                if c >= 1:
                    act.wait_ge(sm["ff1_done"], 2 * c)
                nc.scalar.activation(hT[:, :], MB[:, S:2 * S], ACT.Identity, bias=col(BETA2), scale=col(G2)
                                     ).then_inc(sm["hT_ready"], 1)

            def th_out(c, j):
                act.wait_ge(sm["u_ready"], 2 * c + j + 1)
                if c >= 1:
                    act.wait_ge(sm["g_ready"], 2 * (c - 1) + j + 1)
                nc.scalar.activation(th[:, 2 * j:2 * j + 2, :], u[:, 2 * j:2 * j + 2, :], ACT.Tanh,
                                     scale=0.851).then_inc(sm["th_ready"], 1)

            def x3_out(c):
                act.wait_ge(sm["ff2_done"], c + 1)
                nc.scalar.activation(x3T[:, c, :], MA[:, 0:S], ACT.Identity, bias=col(B2)
                                     ).then_inc(sm["x3_ready"], 1)

            def hid_out(c):
                act.wait_ge(sm["dn_done"], c + 1)
                nc.scalar.activation(hid[:, c, :], MA[0:A, S:2 * S], ACT.Identity, bias=col(DOWNB, 1, A)
                                     ).then_inc(sm["hid_ready"], 1)

            def gelu(j):
                for b in (2 * j, 2 * j + 1):
                    act.wait_ge(sm["hid_ready"], b + 1)
                    nc.scalar.activation(ghid[:, b, :], hid[:, b, :], ACT.Gelu).then_inc(sm["ghid_ready"], 1)

            def eo_out(j):
                act.wait_ge(sm["eo_done"], j + 1)
                act.wait_ge(sm["ctx_done"], NG * B)
                for b in (2 * j, 2 * j + 1):
                    nc.scalar.activation(eoT[0:A, b, :], EB[j][0:A, (b % 2) * S:(b % 2 + 1) * S], ACT.Identity,
                                         bias=bsel[:, b:b + 1]).then_inc(sm["eo_ready"], 1)

            table = {0: [(x1T_out, -1)], 2: [(hT_out, 2), (qk_out, -1)],
                     6: [(lambda c: th_out(c, 0), 2)], 7: [(lambda c: th_out(c, 1), 2)],
                     9: [(mask_bias, -1)], 10: [(ctxT_out, 1), (x3_out, 2)],
                     12: [(x2_out, 1), (hid_out, 2)]}
            tail = {(B, 5): [(gelu, 0), (gelu, 1)], (B, 8): [(gelu, 2)], (B, 11): [(eo_out, 0)],
                    (B, 12): [(eo_out, 1), (eo_out, 2)], (B + 1, 13): [(gelu, 3), (eo_out, 3)]}
            for n in STEPS:
                for h in range(H):
                    t = turning(n, h)
                    if t is not None:
                        probs(*t)
                    w = using(n, h)
                    if w is not None and w[1] % 2 == 1:
                        ctxA_out(w[0], w[1] // 2)
                    for f, back in table.get(h, []):
                        c = item(n, back)
                        if c is not None:
                            f(c)
                    for f, j in tail.get((n, h), []):
                        f(j)

        @block.vector
        def _(dve):
            def stats1(t0, t1):
                for t in range(t0, t1):
                    if t % QT == 0:
                        dve.wait_ge(x_in[t // QT], 16)
                    nc.vector.bn_stats(st1[:, t, :], x_sb[:, t // QT, t % QT, :]).then_inc(sm["stats1"], 1)
                for t in range(t0, t1):
                    dve.wait_ge(sm["stats1"], t0 + t + 1)
                    nc.vector.bn_aggr(mv1[:, t, :], st1[:, t, :]).then_inc(sm["stats1"], 1)

            stats1(0, QT)
            newton_seed(dve, mv1[:, 0:QT, 1], nt1[:, :, 0:QT], sm["stats1"], sm["y1_seed"], 2 * QT, 0, QT)
            newton_steps(dve, nt1[:, :, 0:QT], sm["y1_seed"], NSEED, sm["nt1_step"], 0)
            nc.vector.memset(vaug[:, :, :, :, :], 0.0).then_inc(sm["ones_set"], 1)
            dve.wait_ge(sm["ones_set"], 1)
            nc.vector.memset(vaug[:, :, :, :, HD:HD + 1], 1.0).then_inc(sm["ones_set"], 1)

            dve.wait_ge(sm["t_in"], 16)
            dve.wait_ge(sm["cols_in"], 16)
            nc.vector.tensor_copy(emb[:, 0, :], emb_i[:, :]).then_inc(sm["emb_x"], 1)
            dve.wait_ge(sm["emb_x"], 1)
            nc.vector.tensor_scalar(emb[:, 1, :], emb[:, 0, :], RESCALE / STEPS_T, None, ALU.mult
                                    ).then_inc(sm["emb_x"], 1)
            dve.wait_ge(sm["emb_x"], 2)
            nc.vector.tensor_scalar(emb[:, 0, :], emb[:, 1, :], col(FREQ), None, ALU.mult
                                    ).then_inc(sm["emb_x"], 1)
            dve.wait_ge(sm["emb_x"], 3)
            chain = [0]

            def link(ins, s="emb_silu"):
                chain[0] += 1
                ins.then_inc(sm[s], 1)
                dve.wait_ge(sm[s], chain[0])

            link(nc.vector.tensor_scalar(emb[:, 1, :], emb[:, 0, :], 1.0 / 6.283185307179586, col(PHASE),
                                         ALU.mult, ALU.add))
            link(nc.vector.tensor_scalar(emb[:, 2, :], emb[:, 1, :], ROUND, ROUND, ALU.add, ALU.subtract))
            for tau in (TAU1, TAU2, TAU3):
                link(nc.vector.scalar_tensor_tensor(emb[:, 0, :], emb[:, 2, :], -tau, emb[:, 0, :],
                                                    ALU.mult, ALU.add))
            nc.vector.tensor_scalar(emb[:, 1, :], col(PHASE).to_broadcast([P, B]), 6.283185307179586, None,
                                    ALU.mult).then_inc(sm["emb_x"], 1)
            dve.wait_ge(sm["emb_x"], 4)
            nc.vector.tensor_tensor(out=emb[:, 5, :], in0=emb[:, 0, :], in1=emb[:, 1, :], op=ALU.add
                                    ).then_inc(sm["emb_x"], 1)
            dve.wait_ge(sm["emb_x"], 5)
            nc.vector.tensor_scalar(emb[:, 2, :], emb[:, 5, :], 3.1415925, -3.1415925, ALU.min, ALU.max
                                    ).then_inc(sm["emb_x"], 1)

            def norm1(b):
                if b >= 2:
                    dve.wait_ge(sm["t1_done"], b - 1)
                dve.wait_ge(sm["nt1_step"], NSTEP * (1 if b == 0 else 2))
                for t in range(QT):
                    k = b * QT + t
                    last = nc.vector.tensor_scalar(z1[:, b % 2, t, :], x_sb[:, b, t, :], mv1[:, k, 0:1],
                                                   nt1[:, 1, k:k + 1], ALU.subtract, ALU.mult)
                last.then_inc(sm["z1_ready"], 1)

            norm1(0)
            dve.wait_ge(sm["emb_exp"], 1)
            link(nc.vector.tensor_scalar(emb[:, 5, :], emb[:, 4, :], 1.0, None, ALU.add))
            link(nc.vector.reciprocal(emb[:, 6, :], emb[:, 5, :]))
            link(nc.vector.tensor_tensor(out=emb[:, 7, :], in0=emb[:, 3, :], in1=emb[:, 6, :], op=ALU.mult))
            dve.wait_ge(sm["ada_mm"], 1)
            nc.vector.tensor_scalar(ada[:, 0, :], MC[:, 0:B], col(BADA_S), 1.0, ALU.add, ALU.add
                                    ).then_inc(sm["ada_ready"], 1)
            nc.vector.tensor_scalar(ada[:, 1, :], MC[:, B:2 * B], col(BADA_H), None, ALU.add
                                    ).then_inc(sm["ada_ready"], 1)
            stats1(QT, B * QT)
            newton_seed(dve, mv1[:, QT:, 1], nt1[:, :, QT:], sm["stats1"], sm["y1_seed"],
                        2 * B * QT, NSEED, (B - 1) * QT)
            newton_steps(dve, nt1[:, :, QT:], sm["y1_seed"], 2 * NSEED, sm["nt1_step"], ROUNDS)

            dve.wait_ge(sm["dom_in"], 16)
            E1 = A + 1
            dchain = [0]

            def dlink(ins):
                dchain[0] += 1
                ins.then_inc(sm["dom_ready"], 1)
                dve.wait_ge(sm["dom_ready"], dchain[0])

            dlink(nc.vector.tensor_copy(dom[:, 0, :], dom_i[:, :]))
            dlink(nc.vector.tensor_scalar(dom[:, 1, :], dom[:, 0, :], 0.0, float(NE - 1), ALU.max, ALU.min))
            dlink(nc.vector.tensor_tensor(out=dom[:, 2, :], in0=dom[:, 0, :], in1=dom[:, 1, :],
                                          op=ALU.is_equal))
            dlink(nc.vector.tensor_scalar(dom[:, 3, :], dom[:, 1, :], col(ECOL, 1, E1), None, ALU.is_equal))
            dlink(nc.vector.tensor_tensor(out=dom[:, 4, :], in0=dom[:, 3, :], in1=dom[:, 2, :], op=ALU.mult))
            dlink(nc.vector.tensor_scalar(dom[A:E1, 4, :], dom[A:E1, 2, :], -1.0, 1.0, ALU.mult, ALU.add))
            assert dchain[0] == 6
            dve.wait_ge(sm["wsel_mm"], 1)
            nc.vector.tensor_copy(wsel[:, :, :].rearrange("a b o -> a o b"),
                                  MC[0:A, 0:A * B].rearrange("a (o b) -> a o b", b=B)
                                  ).then_inc(sm["wsel_ready"], 1)
            nc.vector.tensor_copy(bsel[:, :], MC[0:A, A * B:A * B + B]).then_inc(sm["wsel_ready"], 1)

            def scores(n, h):
                r = (n * NG + h // G) % RING
                dve.wait_ge(sm["scores_done"], H * n + h + 1)
                if h % G == 0:
                    dve.wait_ge(f_in[r], 16 * ((n * NG + h // G) // RING + 1))
                if h == 0 and n >= 2:
                    dve.wait_ge(sm["nan_ready"], n - 1)
                for t in range(QT):
                    last = nc.vector.tensor_tensor_reduce(
                        out=F[:, r, h % G, t, :], in0=SB[h % 2][:, t * S:(t + 1) * S], in1=F[:, r, h % G, t, :],
                        scale=1.0, scalar=-3.4e38, op0=ALU.add, op1=ALU.max,
                        accum_out=mx[:, n % 2, t, h:h + 1])
                last.then_inc(sm["scores_read"], 1)

            def center(n, h):
                r = (n * NG + h // G) % RING
                dve.wait_ge(sm["scores_read"], H * n + h + 1)
                for t in range(QT):
                    z = F[:, r, h % G, t, :]
                    last = nc.vector.tensor_scalar(z, z, mx[:, n % 2, t, h:h + 1], None, ALU.subtract)
                last.then_inc(sm["even_centered"], 1)

            def v_out(b):
                dve.wait_ge(sm["vp_done"], b + 1)
                dve.wait_ge(sm["rows_in"], 16)
                dve.wait_ge(sm["ones_set"], 2)
                if b >= 2:
                    dve.wait_ge(sm["ctx_done"], NG * (b - 1))
                for t in range(QT):
                    last = nc.vector.tensor_tensor(
                        out=vaug[:, b % 2, t, :, 0:HD],
                        in0=MA[:, t * D:(t + 1) * D].rearrange("p (h d) -> p h d", h=H),
                        in1=rows_sb[:, 0, :].rearrange("p (h d) -> p h d", h=H), op=ALU.add)
                last.then_inc(sm["v_ready"], 1)

            def norm_ctx(c):
                dve.wait_ge(sm["tc_done"], 2 * (c + 1))
                dve.wait_ge(sm["nan_ready"], c + 1)
                if c >= 1:
                    dve.wait_ge(sm["tc2_done"], c)
                tb = [MB[:, :].rearrange("p (h e) -> p h e", h=H), MC[:, :].rearrange("p (h e) -> p h e", h=H)]
                for t in range(QT):
                    last = nc.vector.tensor_tensor(out=csum[:, t, :], in0=tb[t][:, :, HD],
                                                   in1=nanfix[:, c % 2, t, :], op=ALU.add)
                last.then_inc(sm["rsum_fixed"], 1)
                dve.wait_ge(sm["rsum_fixed"], c + 1)
                nc.vector.reciprocal(csum[:, :, :], csum[:, :, :]).then_inc(sm["rsum_inv"], 1)
                dve.wait_ge(sm["rsum_inv"], c + 1)
                for t in range(QT):
                    last = nc.vector.tensor_tensor(
                        out=ctxn[:, t, :].rearrange("p (h d) -> p h d", h=H), in0=tb[t][:, :, 0:HD],
                        in1=csum[:, t, :].unsqueeze(2).to_broadcast([P, H, HD]), op=ALU.mult)
                last.then_inc(sm["ctxn_ready"], 1)

            def stats2(c):
                dve.wait_ge(sm["x2_ready"], c + 1)
                if c >= 1:
                    dve.wait_ge(sm["z2_ready"], c)
                for t in range(QT):
                    nc.vector.bn_stats(st2[:, t, :], x2[:, c % 2, t, :]).then_inc(sm["stats2"], 1)
                for t in range(QT):
                    dve.wait_ge(sm["stats2"], 2 * QT * c + QT + t)
                    nc.vector.bn_aggr(mv2[:, c % 2, t, :], st2[:, t, :]).then_inc(sm["stats2"], 1)
                newton_seed(dve, mv2[:, c % 2, :, 1], nt2, sm["stats2"], sm["y2_seed"], 2 * QT * (c + 1),
                            NSEED * c, QT)

            def round2(c, r):
                if r == 0:
                    dve.wait_ge(sm["y2_seed"], NSEED * (c + 1))
                newton_round(dve, nt2, sm["nt2_step"], ROUNDS * c + r)

            def norm2(c):
                dve.wait_ge(sm["nt2_step"], NSTEP * (c + 1))
                if c >= 1:
                    dve.wait_ge(sm["t2_done"], c)
                for t in range(QT):
                    last = nc.vector.tensor_scalar(z2[:, t, :], x2[:, c % 2, t, :], mv2[:, c % 2, t, 0:1],
                                                   nt2[:, 1, t:t + 1], ALU.subtract, ALU.mult)
                last.then_inc(sm["z2_ready"], 1)

            def u_out(c, j):
                dve.wait_ge(sm["ff1_done"], 2 * c + j + 1)
                if c >= 1:
                    dve.wait_ge(sm["ff2_done"], c)
                nc.vector.tensor_tensor(out=u[:, 2 * j:2 * j + 2, :],
                                        in0=(MB, MC)[j][:, :].rearrange("p (f s) -> p f s", f=2),
                                        in1=col(B1 + 2 * j, 2).unsqueeze(2).to_broadcast([P, 2, S]),
                                        op=ALU.add).then_inc(sm["u_ready"], 1)

            def halve_w2(n):
                dve.wait_ge(sm["w2_in"], 16)
                nc.vector.tensor_scalar(W2, W2, 0.5, None, ALU.mult).then_inc(sm["w2_halved"], 1)

            def g_out(c, j):
                dve.wait_ge(sm["th_ready"], 2 * c + j + 1)
                uu = u[:, 2 * j:2 * j + 2, :]
                nc.vector.scalar_tensor_tensor(uu, th[:, 2 * j:2 * j + 2, :], 1.0, uu, ALU.add, ALU.mult
                                               ).then_inc(sm["g_ready"], 1)

            def qk_part2(b):
                dve.wait_ge(sm["rest_ready"], b + 1)
                nc.vector.tensor_copy(parts[:, :, 1, :], qk_rest[:, :, :]).then_inc(sm["part2_ready"], 1)

            def norm3(q):
                dve.wait_ge(sm["up_done"], q + 1)
                for t in range(4):
                    nc.vector.bn_stats(st3[:, 4 * q + t, :], UB[q][:, t * D:(t + 1) * D]
                                       ).then_inc(sm["st3_step"], 1)
                for t in range(4):
                    dve.wait_ge(sm["st3_step"], 8 * q + 4 + t)
                    nc.vector.bn_aggr(mv3[:, 4 * q + t, :], st3[:, 4 * q + t, :]).then_inc(sm["st3_step"], 1)
                nt = nt3[:, :, 4 * q:4 * q + 4]
                newton_seed(dve, mv3[:, 4 * q:4 * q + 4, 1], nt, sm["st3_step"], sm["y3_seed"], 8 * (q + 1),
                            NSEED * q, 4)
                newton_steps(dve, nt, sm["y3_seed"], NSEED * (q + 1), sm["nt3_step"], ROUNDS * q)
                dve.wait_ge(sm["nt3_step"], NSTEP * (q + 1))
                for t in range(4):
                    i = 4 * q + t
                    nc.vector.tensor_scalar(y[:, i // QT, i % QT, :], UB[q][:, t * D:(t + 1) * D],
                                            mv3[:, i, 0:1], nt3[:, 1, i:i + 1], ALU.subtract, ALU.mult
                                            ).then_inc(sm["norm3_ready"], 1)

            table = {0: [(norm2, 2)], 4: [(lambda c: u_out(c, 0), 2)],
                     5: [(lambda c: u_out(c, 1), 2), (qk_part2, -1)],
                     6: [(v_out, 0)], 7: [(lambda c: g_out(c, 0), 2)], 8: [(lambda c: g_out(c, 1), 2)],
                     9: [(norm_ctx, 1)], 12: [(stats2, 1), (norm1, -2)], 13: [(lambda c: round2(c, 0), 1)],
                     14: [(lambda c: round2(c, 1), 1)], 15: [(lambda c: round2(c, 2), 1)]}
            tail = {(0, 15): [(halve_w2, 0)], (B + 1, 1): [(norm3, 0)], (B + 1, 3): [(norm3, 1)],
                    (B + 1, 6): [(norm3, 2)], (B + 1, 13): [(norm3, 3)]}
            for n in STEPS:
                for h in range(H):
                    c = item(n, 0)
                    if c is not None:
                        scores(c, h)
                        if h % 2 == 1:
                            center(c, h - 1)
                    for f, back in table.get(h, []):
                        c = item(n, back)
                        if c is not None:
                            f(c)
                    for f, j in tail.get((n, h), []):
                        f(j)

        @block.tensor
        def _(pe):
            mm = nc.tensor.matmul

            def turn(dst, src, start=True, stop=True):
                return mm(dst, src, idf[:, :], start=start, stop=stop, is_transpose=True)

            def turn_z1(b):
                pe.wait_ge(sm["z1_ready"], b + 1)
                if b == 0:
                    pe.wait_ge(sm["idf_in"], 16)
                if b >= 2:
                    pe.wait_ge(sm["v_ready"], b - 1)
                if b >= 4:
                    pe.wait_ge(sm["hid_ready"], b - 3)
                for t in range(QT):
                    last = turn(MA[:, t * P:(t + 1) * P], z1[:, b % 2, t, :])
                last.then_inc(sm["t1_done"], 1)

            def project_qk(b):
                pe.wait_ge(sm["x1T_ready"], b + 1)
                mm(MA[:, 0:S], WQ, x1T[:, b, :], start=True, stop=True)
                mm(MA[:, S:2 * S], WK, x1T[:, b, :], start=True, stop=True).then_inc(sm["qkp_done"], 1)

            def project_v(b):
                pe.wait_ge(sm["qk_ready"], 4 * min(b + 2, B))
                for t in range(QT):
                    last = mm(MA[:, t * D:(t + 1) * D], x1T[:, b, t * P:(t + 1) * P], WV, start=True, stop=True)
                last.then_inc(sm["vp_done"], 1)

            def score(n, h):
                bank = SB[h % 2]
                if h == 0:
                    pe.wait_ge(sm["maskb_ready"], n + 1)
                    pe.wait_ge(q_in[n % 2], 16 * (n // 2 + 1))
                    pe.wait_ge(k_in[n % 2], 16 * NPARTS * (n // 2 + 1))
                    if n == 0:
                        pe.wait_ge(sm["idb_in"], 16)
                if H * n + h >= 2:
                    pe.wait_ge(sm["scores_read"], H * n + h - 1)
                mm(bank[:, :], idb[:, :], maskb[:, n % 2, :, :].rearrange("p t s -> p (t s)"),
                   start=True, stop=False)
                for t in range(QT):
                    last = mm(bank[:, t * S:(t + 1) * S], qstack[:, n % 2, h, t * P:(t + 1) * P],
                              kstack[:, n % 2, h, :], start=False, stop=(t == QT - 1))
                last.then_inc(sm["scores_done"], 1)

            def turn_scores(c, h):
                k = H * c + h
                bank = ZB[k % 2]
                pe.wait_ge(sm["odd_centered" if h % 2 else "even_centered"], k // 2 + 1)
                if k >= 2:
                    pe.wait_ge(sm["probs_ready"], k - 1)
                r = (c * NG + h // G) % RING
                for kt in range(QT):
                    for t in range(QT):
                        last = turn(bank[:, kt * S + t * P:kt * S + (t + 1) * P],
                                    F[:, r, h % G, t, kt * P:(kt + 1) * P])
                last.then_inc(sm["turned"], 1)

            def context(c, g):
                pe.wait_ge(sm["probs_ready"], H * c + G * (g + 1))
                if g == 0:
                    pe.wait_ge(sm["v_ready"], c + 1)
                if g % 2 == 0 and NG * c + g >= 2:
                    pe.wait_ge(sm["ctxA_ready"], (NG * c + g) // 2)
                for kt in range(QT):
                    for j in range(G):
                        h = G * g + j
                        last = mm(CB[32 * j:32 * j + 32, (g % 2) * S:(g % 2 + 1) * S],
                                  vaug[:, c % 2, kt, h, :], PT[:, (H * c + h) % NPT, kt, :],
                                  start=(kt == 0), stop=(kt == QT - 1))
                last.then_inc(sm["ctx_done"], 1)

            def turn_ctx(c):
                pe.wait_ge(sm["ctxA_ready"], 2 * (c + 1))
                if c == 0:
                    pe.wait_ge(sm["wsel_ready"], 2)
                else:
                    pe.wait_ge(sm["u_ready"], 2 * c)
                for t in range(QT):
                    for g in range(NG):
                        last = turn((MB, MC)[t][:, g * P:(g + 1) * P], ctxA[:, g, t * P:(t + 1) * P])
                    last.then_inc(sm["tc_done"], 1)

            def turn_ctxn(c):
                pe.wait_ge(sm["ctxn_ready"], c + 1)
                for t in range(QT):
                    last = turn(MB[:, t * P:(t + 1) * P], ctxn[:, t, :])
                last.then_inc(sm["tc2_done"], 1)

            def out_project(c):
                pe.wait_ge(sm["ctxT_ready"], c + 1)
                if c == 0:
                    pe.wait_ge(sm["bo_in"], 16)
                    pe.wait_ge(sm["pads_set"], 1)
                for t in range(QT):
                    o = MC[:, t * D:(t + 1) * D]
                    mm(o, ctxT[:, t * P:(t + 1) * P], WO, start=True, stop=False)
                    mm(o, ones_row[:, :], bo_sb[:, :], start=False, stop=False)
                    last = turn(o, x1T[:, c, t * P:(t + 1) * P], start=False, stop=True)
                last.then_inc(sm["o_done"], 1)

            def turn_z2(c):
                pe.wait_ge(sm["z2_ready"], c + 1)
                for t in range(QT):
                    last = turn(MB[:, S + t * P:S + (t + 1) * P], z2[:, t, :])
                last.then_inc(sm["t2_done"], 1)

            def ff1(c, j):
                if j == 0:
                    pe.wait_ge(sm["hT_ready"], c + 1)
                else:
                    pe.wait_ge(sm["x2_ready"], c + 1)
                for i in range(2):
                    f = 2 * j + i
                    last = mm((MB, MC)[j][:, i * S:(i + 1) * S], W1[:, f * P:(f + 1) * P], hT[:, :],
                              start=True, stop=True)
                last.then_inc(sm["ff1_done"], 1)

            def ff2(c):
                pe.wait_ge(sm["g_ready"], 2 * (c + 1))
                if c == 0:
                    pe.wait_ge(sm["w2_halved"], 1)
                pe.wait_ge(sm["v_ready"], min(c + 3, B))
                for f in range(FF):
                    mm(MA[:, 0:S], W2[:, f * P:(f + 1) * P], u[:, f, :], start=(f == 0), stop=False)
                for t in range(QT):
                    last = turn(MA[:, t * P:(t + 1) * P], x2[:, c % 2, t, :], start=False, stop=(t == QT - 1))
                last.then_inc(sm["ff2_done"], 1)

            def down_project(c):
                pe.wait_ge(sm["x3_ready"], c + 1)
                if c == 0:
                    pe.wait_ge(sm["down_in"], 16)
                mm(MA[0:A, S:2 * S], down_sb[:, :], x3T[:, c, :], start=True, stop=True).then_inc(sm["dn_done"], 1)

            pe.wait_ge(sm["w_in"], 16)
            pe.wait_ge(sm["emb_silu"], 8)
            mm(MC[:, 0:B], WADA[:, 0:D], emb[:, 7, :], start=True, stop=True)
            mm(MC[:, B:2 * B], WADA[:, D:2 * D], emb[:, 7, :], start=True, stop=True).then_inc(sm["ada_mm"], 1)
            turn_z1(0)
            project_qk(0)
            pe.wait_ge(sm["expert_in"], 16)
            pe.wait_ge(sm["dom_ready"], 6)
            pe.wait_ge(sm["ada_ready"], 2)
            for o in range(A):
                mm(MC[0:A, o * B:(o + 1) * B], expert_sb[:, o * A:(o + 1) * A], dom[:, 4, :],
                   start=True, stop=True)
            mm(MC[0:A, A * B:A * B + B], expert_sb[:, A * A:A * A + A], dom[:, 4, :], start=True, stop=False)
            mm(MC[0:A, A * B:A * B + B], expert_sb[:, A * A + A:A * A + 2 * A], dom[:, 3, :],
               start=False, stop=True).then_inc(sm["wsel_mm"], 1)

            def expert(j):
                if j == 0:
                    pe.wait_ge(sm["probs_ready"], H * B)
                if j == 1:
                    pe.wait_ge(sm["ctxA_ready"], 2 * B)
                if j >= 2:
                    pe.wait_ge(sm["eo_ready"], (2, 6)[j - 2])
                for b in (2 * j, 2 * j + 1):
                    pe.wait_ge(sm["ghid_ready"], b + 1)
                    last = mm(EB[j][0:A, (b % 2) * S:(b % 2 + 1) * S], wsel[:, b, :], ghid[:, b, :],
                              start=True, stop=True)
                last.then_inc(sm["eo_done"], 1)

            def up_project(j):
                if j == 0:
                    pe.wait_ge(sm["up_in"], 16)
                    pe.wait_ge(sm["pads_set"], 2)
                    pe.wait_ge(sm["scores_read"], H * B)
                if j == 2:
                    pe.wait_ge(sm["probs_ready"], H * B)
                for b in (2 * j, 2 * j + 1):
                    pe.wait_ge(sm["eo_ready"], b + 1)
                    for t in range(QT):
                        o = UB[j][:, (b % 2 * QT + t) * D:(b % 2 * QT + t + 1) * D]
                        mm(o, eoT[:, b, t * P:(t + 1) * P], up_sb[:, :], start=True, stop=False)
                        last = turn(o, x3T[:, b, t * P:(t + 1) * P], start=False, stop=True)
                last.then_inc(sm["up_done"], 1)

            table = {0: [(turn_z1, -1)], 2: [(turn_z2, 2), (project_qk, -1)], 4: [(lambda c: ff1(c, 0), 2)],
                     5: [(project_v, 0), (lambda c: ff1(c, 1), 2)], 8: [(turn_ctx, 1)], 10: [(turn_ctxn, 1), (ff2, 2)],
                     12: [(out_project, 1), (down_project, 2)]}
            tail = {(B, 9): [(expert, 0), (expert, 1)],
                    (B, 12): [(expert, 2), (up_project, 0), (up_project, 1)], (B, 15): [(up_project, 2)],
                    (B + 1, 13): [(expert, 3), (up_project, 3)]}
            for n in STEPS:
                for h in range(H):
                    c = item(n, 0)
                    if c is not None:
                        score(c, h)
                    t = turning(n, h)
                    if t is not None:
                        turn_scores(*t)
                    w = using(n, h)
                    if w is not None:
                        context(*w)
                    for f, back in table.get(h, []):
                        c = item(n, back)
                        if c is not None and not (f in (turn_z1, project_qk) and c == 0):
                            f(c)
                    for f, j in tail.get((n, h), []):
                        f(j)


def kernel(**inputs):
    import math
    import ml_dtypes
    import numpy as np
    import concourse.bacc as bacc
    from concourse import mybir
    from concourse.bass_utils import run_bass_kernel_spmd

    a = {k: np.asarray(v) for k, v in inputs.items()}
    f32 = np.float32
    B, S, D = a["x"].shape
    H = a["fside_Bx16xSxS_0"].shape[1]
    A = a["L1_cond_down_W"].shape[0]
    NE = a["L1_cond_expert_W"].shape[0]
    P, half = 128, D // 2
    freqs = np.exp(np.arange(half, dtype=f32) * f32(-math.log(10000.0) / (half - 1))).astype(f32)
    freq = np.concatenate([freqs, freqs])
    phase = np.concatenate([np.zeros(half, f32), np.full(half, 0.25, f32)])
    ecol = np.full(P, -1.0, f32)
    ecol[:NE] = np.arange(NE)
    L0 = lambda n: a["L0_cond_" + n]
    L1 = lambda n: a["L1_cond_" + n]
    w2 = L0("W2").reshape(4, P, D).transpose(1, 0, 2).reshape(P, 4 * D)
    wts = np.concatenate([L0("Wq"), L0("Wk"), L0("Wv"), L0("Wo"), L0("W_ada"), L0("W1"), w2], axis=1)
    downb = np.zeros(P, f32)
    downb[:A] = L1("down_b")
    cols = np.stack([L0("b_ada")[:D], L0("b_ada")[D:], L0("bq"), L0("bk"), L0("g2"), L0("beta2"), L0("b2"),
                     freq, phase, ecol, downb, *L0("b1").reshape(4, P)], axis=1)
    rows = np.stack([L0("bv"), L1("ln_gamma"), L1("ln_beta")])
    expert = np.zeros((A + 1, A * A + 2 * A), f32)
    expert[:NE, :A * A] = L1("expert_W").reshape(NE, A * A)
    expert[A, :A * A] = np.eye(A, dtype=f32).reshape(-1)
    expert[:NE, A * A:A * A + A] = L1("expert_b")
    expert[:NE, A * A + A:] = L1("domain_emb")
    up = np.concatenate([L1("up_W").T, L1("up_b")[None, :]], axis=0)
    arrays = {
        "x": a["x"], "tstep": a["itok_B_34_63"], "fside": a["fside_Bx16xSxS_0"], "domain": a["itok_B_0_15"],
        "mask": a["mask_Bx1xSxS_bk0"], "wts": wts, "cols": cols, "rows": rows,
        "bo": L0("bo")[None, :], "down": L1("down_W").T, "up": up, "expert": expert,
        "identf": np.eye(P, dtype=f32), "identb": np.eye(P, dtype=f32).astype(ml_dtypes.bfloat16),
    }
    nc = bacc.Bacc("TRN2", target_bir_lowering=False, num_devices=1)
    named, args = {}, []
    for name, v in arrays.items():
        v = np.ascontiguousarray(v)
        named[f"in_{name}"] = v
        args.append(nc.dram_tensor(f"in_{name}", v.shape, mybir.dt.from_np(v.dtype), kind="ExternalInput").ap())
    args.append(nc.dram_tensor("out_0", (B, S, D), mybir.dt.float32, kind="ExternalOutput").ap())
    cond_seq_kernel(nc, *args)
    r = run_bass_kernel_spmd(nc, [named], core_ids=[0])
    return r.results[0]["out_0"]
```

```python
import concourse.bass as bass
from concourse import mybir
from contextlib import ExitStack


def cond_seq_kernel(nc, x, tstep, fside, domain, mask, wts, cols, rows, bo, down, up, expert,
                    identf, identb, out):
    fp32 = mybir.dt.float32
    bf16 = mybir.dt.bfloat16
    i32 = mybir.dt.int32
    u8 = mybir.dt.uint8
    ALU = mybir.AluOpType
    ACT = mybir.ActivationFunctionType

    B, S, D = x.shape
    H = fside.shape[1]
    HD = D // H
    P = 128
    QT = S // P
    FF = 4
    A = down.shape[1]
    NE = 16
    G = 4
    NG = H // G
    QS = float(HD) ** -0.5
    EPS = 1e-5
    MASKED = -3.0e38
    RING = 8
    NPT = 8
    NPARTS = 3
    KROWS = NPARTS * NPARTS * HD
    LAG = 4
    VHEADS = [h for h in range(0, H, 2) if h != 12]
    TAU1 = 6.28125
    TAU2 = 0.0019350051879882812
    TAU3 = 6.283185307179586 - TAU1 - TAU2
    RESCALE, STEPS_T = 4000.0, 100.0
    ROUND = 12582912.0
    ROUNDS = 3
    MAGIC = float(0x5F3759DF)

    parts_dram = nc.dram_tensor("parts_dram", [2, 2, NPARTS, HD, H, S], bf16).ap()

    ctx = ExitStack()
    with ctx:
        def sb(name, shape, dt=fp32):
            return ctx.enter_context(nc.sbuf_tensor(name, shape, dt))

        def sem(name):
            return ctx.enter_context(nc.semaphore(name))

        wts_sb = sb("wts_sb", [P, wts.shape[1]])
        WQ, WK, WV, WO = (wts_sb[:, i * D:(i + 1) * D] for i in range(4))
        WADA = wts_sb[:, 4 * D:6 * D]
        W1 = wts_sb[:, 6 * D:6 * D + FF * P]
        W2 = wts_sb[:, 6 * D + FF * P:6 * D + 2 * FF * P]
        cols_sb = sb("cols_sb", [P, cols.shape[1]])
        (BADA_S, BADA_H, BQ, BK, G2, BETA2, B2, FREQ, PHASE, ECOL, DOWNB) = range(11)
        B1 = 11

        def col(i, n=1, p=P):
            return cols_sb[0:p, i:i + n]

        rows_sb = sb("rows_sb", [P, 3, D])
        bo_sb = sb("bo_sb", [1, D])
        down_sb = sb("down_sb", [P, A])
        up_sb = sb("up_sb", [A + 1, D])
        idf = sb("idf", [P, P])
        idb = sb("idb", [P, P], bf16)
        ones_row = sb("ones_row", [1, P])

        x_sb = sb("x_sb", [P, B, QT, D])
        st1 = sb("st1", [P, B * QT, 6])
        mv1 = sb("mv1", [P, B * QT, 2])
        nt1 = sb("nt1", [P, 4, B * QT])
        z1 = sb("z1", [P, 2, QT, D])
        x1T = sb("x1T", [P, B, S])
        qkf = sb("qkf", [P, 2, S])
        parts = sb("parts", [P, 2, NPARTS, S], bf16)
        qk_rest = sb("qk_rest", [P, 2, S])
        qstack = sb("qstack", [P, 2, H, S], bf16)
        kstack = sb("kstack", [P, 2, H, S], bf16)
        vaug = sb("vaug", [P, 2, QT, H, 32])
        mask_sb = sb("mask_sb", [P, 2, QT, S], u8)
        maskb = sb("maskb", [P, 2, QT, S], bf16)
        F = sb("F", [P, RING, G, QT, S])
        mx = sb("mx", [P, 2, QT, H])
        nanfix = sb("nanfix", [P, 2, QT, H])
        PT = sb("PT", [P, NPT, QT, S])
        ctxA = sb("ctxA", [P, NG, S])
        csum = sb("csum", [P, QT, H])
        ctxn = sb("ctxn", [P, QT, D])
        ctxT = sb("ctxT", [P, S])
        x2 = sb("x2", [P, 2, QT, D])
        st2 = sb("st2", [P, QT, 6])
        mv2 = sb("mv2", [P, 2, QT, 2])
        nt2 = sb("nt2", [P, 4, QT])
        z2 = sb("z2", [P, QT, D])
        hT = sb("hT", [P, S])
        u = sb("u", [P, FF, S])
        th = sb("th", [P, FF, S])
        x3T = sb("x3T", [P, B, S])
        hid = sb("hid", [A, B, S])
        ghid = hid
        expert_sb = PT[0:A + 1, :, :, :].rearrange("p n t s -> p (n t s)")[:, 0:expert.shape[1]]
        eoT = PT[0:A + 1, 0:4, :, :].rearrange("p n t s -> p (n t) s")
        emb = sb("emb", [P, 8, B])
        emb_i = sb("emb_i", [P, B], i32)
        dom_i = sb("dom_i", [A + 1, B], i32)
        dom = sb("dom", [A + 1, 6, B])
        ada = sb("ada", [P, 2, B])
        qbias = sb("qbias", [P, 1])
        wsel = sb("wsel", [A, B, A])
        bsel = sb("bsel", [A, B])
        st3 = sb("st3", [P, B * QT, 6])
        mv3 = sb("mv3", [P, B * QT, 2])
        nt3 = sb("nt3", [P, 4, B * QT])
        nmr3 = sb("nmr3", [P, B * QT])
        y = x_sb

        banks = [ctx.enter_context(nc.psum_tensor(f"bank{i}", [P, 512], fp32)) for i in range(8)]
        SB = banks[0:2]
        ZB = banks[2:4]
        CB = banks[4]
        MA, MB, MC = banks[5:8]

        GROUPS = [(i, i + 1) for i in range(0, B - 2, 2)] + [(B - 2,), (B - 1,)]
        NE3 = B - 2
        EB = ZB[0]
        UB = [ZB[1], SB[0], SB[1], CB, MB]

        def turned_ctx_banks(c):
            return SB if c == B - 1 else (MB, MC)

        names = """w_in w2_in w2_halved cols_in rows_in bo_in down_in up_in expert_in idf_in idb_in
            t_in dom_in ones_set pads_set stack_pads_set
            emb_x emb_sin emb_exp emb_silu ada_mm ada_ready dom_ready wsel_mm wsel_ready
            stats1 y1_seed nt1_step z1_ready t1_done x1T_ready qkp_done qk_ready rest_ready part2_ready parts_ready
            vp_done v_ready maskb_ready scores_done scores_read vec_centered pool_centered
            nan_ready turned probs_ready ctx_done ctxA_ready tc_done rsum_fixed rsum_inv
            ctxn_ready tc2_done ctxT_ready o_done x2_ready stats2 y2_seed nt2_step z2_ready
            t2_done hT_ready ff1_done u_ready th_ready g_ready ff2_done x3_ready dn_done hid_ready
            ghid_ready eo_done eo_ready up_done st3_step y3_seed nt3_step y_step y_ready
            nmr_ready y_norm y_norm_v last_step last_ready
            out_done""".split()
        sm = {n: sem(n) for n in names}
        x_in = [sem(f"x_in{i}") for i in range(B)]
        mask_in = [sem(f"mask_in{i}") for i in range(2)]
        f_in = [sem(f"f_in{i}") for i in range(RING)]
        q_in = [sem(f"q_in{i}") for i in range(2)]
        k_in = [sem(f"k_in{i}") for i in range(2)]

        parts_out = [sem(f"parts_out{i}") for i in range(2)]

        block = ctx.enter_context(nc.Block())
        STEPS = range(-1, B + 1)
        def item(n, back):
            return n - back if 0 <= n - back < B else None

        def turning(n, h):
            s = H * n + h - LAG
            return (s // H, s % H) if 0 <= s < B * H else None

        def using(n, h):
            s = H * n + h - LAG - (G - 1) - 2
            return (s // H, s % H // G) if 0 <= s < B * H and s % G == 0 else None

        def newton_seed(dve, mv, nt, stats_sem, seed_sem, v0, s0, n):
            dve.wait_ge(stats_sem, v0)
            nc.vector.tensor_scalar(nt[:, 2, :], mv, EPS, None, ALU.add).then_inc(seed_sem, 1)
            dve.wait_ge(seed_sem, s0 + 1)
            nc.vector.tensor_scalar(nt[:, 0, :], nt[:, 2, :], -0.5, None, ALU.mult).then_inc(seed_sem, 1)
            nc.vector.tensor_scalar(nt[:, 3, :].bitcast(i32), nt[:, 2, :].bitcast(i32), 1, None,
                                    ALU.logical_shift_right).then_inc(seed_sem, 1)
            dve.wait_ge(seed_sem, s0 + 3)
            nc.vector.tensor_scalar(nt[:, 1, :].bitcast(i32), nt[:, 3, :].bitcast(i32), -1.0, MAGIC,
                                    ALU.mult, ALU.add).then_inc(seed_sem, 1)

        def newton_round(dve, nt, step_sem, k):
            if k:
                dve.wait_ge(step_sem, 3 * k)
            nc.vector.tensor_tensor(out=nt[:, 2, :], in0=nt[:, 1, :], in1=nt[:, 1, :],
                                    op=ALU.mult).then_inc(step_sem, 1)
            dve.wait_ge(step_sem, 3 * k + 1)
            nc.vector.tensor_tensor(out=nt[:, 3, :], in0=nt[:, 2, :], in1=nt[:, 0, :],
                                    op=ALU.mult).then_inc(step_sem, 1)
            dve.wait_ge(step_sem, 3 * k + 2)
            nc.vector.scalar_tensor_tensor(nt[:, 1, :], nt[:, 3, :], 1.5, nt[:, 1, :],
                                           ALU.add, ALU.mult).then_inc(step_sem, 1)

        def newton_steps(dve, nt, seed_sem, s0, step_sem, k0):
            dve.wait_ge(seed_sem, s0)
            for r in range(ROUNDS):
                newton_round(dve, nt, step_sem, k0 + r)

        NSTEP = 3 * ROUNDS
        NSEED = 4

        @block.sync
        def _(sp):
            def load_x(b):
                sp.dma_start(x_sb[:, b, :, :], x[b].rearrange("(t p) d -> p t d", p=P)).then_inc(x_in[b], 16)

            def load_mask(b):
                if b >= 2:
                    sp.wait_ge(sm["maskb_ready"], b - 1)
                sp.dma_start(mask_sb[:, b % 2, :, :],
                             mask[b, 0].rearrange("(t p) k -> p t k", p=P)).then_inc(mask_in[b % 2], 16)

            def load_bias(b, g):
                r = (b * NG + g) % RING
                if b >= 2:
                    sp.wait_ge(sm["turned"], H * (b - 2) + G * (g + 1))
                sp.dma_start(F[:, r, :, :, :],
                             fside[b, G * g:G * (g + 1)].rearrange("h (t p) k -> p h t k", p=P)
                             ).then_inc(f_in[r], 16)

            sp.dma_start(emb_i[:, :], tstep.rearrange("(o b) -> o b", o=1).to_broadcast([P, B])
                         ).then_inc(sm["t_in"], 16)
            sp.dma_start(cols_sb[:, :], cols).then_inc(sm["cols_in"], 16)
            load_x(0)
            sp.dma_start(wts_sb[:, :6 * D], wts[:, :6 * D]).then_inc(sm["w_in"], 16)
            sp.dma_start(idf[:, :], identf).then_inc(sm["idf_in"], 16)
            load_mask(0)
            sp.dma_start(idb[:, :], identb).then_inc(sm["idb_in"], 16)
            load_bias(0, 0)
            for b in range(1, B):
                load_x(b)
            sp.dma_start(rows_sb[:, :, :], rows.rearrange("(o r) d -> o r d", o=1).to_broadcast([P, 3, D])
                         ).then_inc(sm["rows_in"], 16)
            sp.dma_start(dom_i[:, :], domain.rearrange("(o b) -> o b", o=1).to_broadcast([A + 1, B])
                         ).then_inc(sm["dom_in"], 16)
            sp.dma_start(expert_sb, expert).then_inc(sm["expert_in"], 16)

            for b in range(B):
                if b >= 1:
                    load_mask(b)
                    load_bias(b, 0)
                else:
                    sp.wait_ge(sm["stack_pads_set"], 1)
                for w in range(2):
                    sp.wait_ge(sm["parts_ready"], 2 * b + w + 1)
                    sp.dma_start(parts_dram[b % 2, w].rearrange("i d h s -> (d h) i s"),
                                 parts[:, w, :, :]).then_inc(parts_out[w], 16)
                if b >= 2:
                    sp.wait_ge(sm["scores_done"], H * (b - 1))
                pq = parts_dram[b % 2, 0].rearrange("i d h s -> (i d) (h s)")
                pk = parts_dram[b % 2, 1].rearrange("j d h s -> j d (h s)")
                sp.wait_ge(parts_out[0], 16 * (b + 1))
                sp.dma_start(qstack[0:KROWS, b % 2, :, :].rearrange("p h s -> p (h s)"),
                             pq.unsqueeze(0).to_broadcast([NPARTS, NPARTS * HD, H * S])
                             ).then_inc(q_in[b % 2], 16)
                sp.wait_ge(parts_out[1], 16 * (b + 1))
                for j in range(NPARTS):
                    sp.dma_start(kstack[j * NPARTS * HD:(j + 1) * NPARTS * HD, b % 2, :, :]
                                 .rearrange("p h s -> p (h s)"),
                                 pk[j].unsqueeze(0).to_broadcast([NPARTS, HD, H * S])
                                 ).then_inc(k_in[b % 2], 16)
                for g in range(1, NG):
                    load_bias(b, g)
                if b == 0:
                    sp.dma_start(wts_sb[:, 6 * D:], wts[:, 6 * D:]).then_inc(sm["w2_in"], 16)
                    sp.dma_start(bo_sb[:, :], bo).then_inc(sm["bo_in"], 16)
                    sp.dma_start(down_sb[:, :], down).then_inc(sm["down_in"], 16)
                    sp.dma_start(up_sb[:, :], up).then_inc(sm["up_in"], 16)

            for q, items in enumerate(GROUPS):
                b0, nb = items[0], len(items)
                if b0 < NE3:
                    sp.wait_ge(sm["y_ready"], q + 1)
                else:
                    sp.wait_ge(sm["last_ready"], QT * (b0 - NE3 + 1))
                sp.dma_start(out[b0:b0 + nb].rearrange("b (t p) d -> p (b t) d", p=P),
                             y[:, b0:b0 + nb, :, :].rearrange("p b t d -> p (b t) d")
                             ).then_inc(sm["out_done"], 16)
            sp.wait_ge(sm["out_done"], 16 * len(GROUPS))

        @block.gpsimd
        def _(pool):
            pool.memset(ones_row[:, :], 1.0).then_inc(sm["pads_set"], 1)
            pool.wait_ge(sm["pads_set"], 1)
            for st in (qstack, kstack):
                last = pool.memset(st[64:P, :, :, :].rearrange("p n h s -> p (n h s)").bitcast(i32), 0)
            last.then_inc(sm["stack_pads_set"], 1)
            pool.wait_ge(sm["stack_pads_set"], 1)
            pool.memset(vaug[:, :, :, :, :], 0.0).then_inc(sm["ones_set"], 1)
            pool.wait_ge(sm["ones_set"], 1)
            pool.memset(vaug[:, :, :, :, HD:HD + 1], 1.0).then_inc(sm["ones_set"], 1)

            def center(n, h):
                r = (n * NG + h // G) % RING
                pool.wait_ge(sm["scores_read"], H * n + h + 1)
                z = F[:, r, h % G, :, :]
                pool.tensor_tensor(out=z, in0=z, in1=mx[:, n % 2, :, h:h + 1].to_broadcast([P, QT, S]),
                                   op=ALU.subtract).then_inc(sm["pool_centered"], 1)

            def nan_fix(n):
                if n >= 2:
                    pool.wait_ge(sm["rsum_fixed"], n - 1)
                pool.tensor_scalar(nanfix[:, n % 2, :, :], mx[:, n % 2, :, :], 2.0, 0.0,
                                   ALU.mult, ALU.mult).then_inc(sm["nan_ready"], 1)

            def qk_rest_out(b):
                pool.wait_ge(sm["qk_ready"], 4 * (b + 1))
                if b >= 1:
                    pool.wait_ge(sm["part2_ready"], b + 1)
                pool.tensor_tensor(out=qk_rest[:, :, :], in0=qkf[:, :, :], in1=parts[:, :, 0, :],
                                   op=ALU.subtract).then_inc(sm["rest_ready"], 1)

            def qk_part3(b, w):
                pool.wait_ge(sm["part2_ready"], b + 2)
                pool.tensor_tensor(out=parts[:, w, 2, :], in0=qk_rest[:, w, :], in1=parts[:, w, 1, :],
                                   op=ALU.subtract).then_inc(sm["parts_ready"], 1)

            def eo_ones(n):
                pool.wait_ge(sm["ctx_done"], NG * B)
                pool.wait_ge(sm["nan_ready"], B)
                pool.memset(eoT[A:A + 1, :, :], 1.0).then_inc(sm["pads_set"], 1)
                pool.wait_ge(sm["pads_set"], 2)

            def gamma_beta(j):
                yt = y[:, 2 * j:2 * j + 2, :, :].rearrange("p b t d -> p (b t) d")
                if j < NE3 // 2 - 1:
                    pool.wait_ge(sm["y_norm"], 2 * QT * (j + 1))
                else:
                    pool.wait_ge(sm["y_norm_v"], 2 * QT)
                pool.tensor_tensor(out=yt, in0=yt, in1=rows_sb[:, 1:2, :].to_broadcast([P, 2 * QT, D]),
                                   op=ALU.mult).then_inc(sm["y_step"], 1)
                pool.wait_ge(sm["y_step"], j + 1)
                pool.tensor_tensor(out=yt, in0=yt, in1=rows_sb[:, 2:3, :].to_broadcast([P, 2 * QT, D]),
                                   op=ALU.add).then_inc(sm["y_ready"], 1)

            table = {3: [(qk_rest_out, -1)], 7: [(lambda b: qk_part3(b, 0), -1)],
                     8: [(lambda b: qk_part3(b, 1), -1)], 15: [(nan_fix, 0)]}
            for n in STEPS:
                for h in range(H):
                    c = item(n, 0)
                    if c is not None and h not in VHEADS:
                        center(c, h)
                    for f, back in table.get(h, []):
                        c = item(n, back)
                        if c is not None and not (f is not nan_fix and c == 0):
                            f(c)
            eo_ones(B)
            for j in range(NE3 // 2):
                gamma_beta(j)

        @block.scalar
        def _(act):
            act.wait_ge(sm["emb_x"], 6)
            nc.scalar.activation(emb[:, 3, :], emb[:, 2, :], ACT.Sin).then_inc(sm["emb_sin"], 1)
            act.wait_ge(sm["emb_sin"], 1)
            nc.scalar.activation(emb[:, 4, :], emb[:, 3, :], ACT.Exp, scale=-1.0).then_inc(sm["emb_exp"], 1)
            act.wait_ge(sm["cols_in"], 16)
            nc.scalar.activation(qbias[:, :], col(BQ), ACT.Copy, scale=QS)

            def x1T_out(b):
                act.wait_ge(sm["t1_done"], b + 1)
                act.wait_ge(sm["ada_ready"], 2)
                nc.scalar.activation(x1T[:, b, :], MA[:, 0:S], ACT.Identity, bias=ada[:, 1, b:b + 1],
                                     scale=ada[:, 0, b:b + 1]).then_inc(sm["x1T_ready"], 1)

            def mask_bias(b):
                act.wait_ge(mask_in[b % 2], 16 * (b // 2 + 1))
                if b >= 2:
                    act.wait_ge(sm["scores_done"], H * (b - 1))
                nc.scalar.activation(maskb[:, b % 2, :, :], mask_sb[:, b % 2, :, :], ACT.Copy,
                                     scale=MASKED).then_inc(sm["maskb_ready"], 1)

            def qk_out(b):
                act.wait_ge(sm["qkp_done"], b + 1)
                if b >= 1:
                    act.wait_ge(sm["rest_ready"], b + 1)
                    for w in range(2):
                        act.wait_ge(parts_out[w], 16 * b)
                for w, bias, scale in ((0, qbias[:, :], QS), (1, col(BK), 1.0)):
                    for dst in (qkf[:, w, :], parts[:, w, 0, :]):
                        nc.scalar.activation(dst, MA[:, w * S:(w + 1) * S], ACT.Identity, bias=bias, scale=scale
                                             ).then_inc(sm["qk_ready"], 1)

            def probs(c, h):
                k = H * c + h
                act.wait_ge(sm["turned"], k + 1)
                if k == 0:
                    act.wait_ge(sm["wsel_mm"], 1)
                if k >= NPT:
                    act.wait_ge(sm["ctx_done"], (k - NPT) // G + 1)
                nc.scalar.activation(PT[:, k % NPT, :, :], ZB[k % 2][:, :].rearrange("p (t q) -> p t q", t=QT),
                                     ACT.Exp).then_inc(sm["probs_ready"], 1)

            def ctxA_out(c, j):
                act.wait_ge(sm["ctx_done"], NG * c + 2 * (j + 1))
                if c >= 1:
                    act.wait_ge(sm["tc_done"], 2 * c)
                nc.scalar.activation(ctxA[:, 2 * j:2 * j + 2, :],
                                     CB[:, :].rearrange("p (g q) -> p g q", g=2), ACT.Copy
                                     ).then_inc(sm["ctxA_ready"], 1)

            def ctxT_out(c):
                act.wait_ge(sm["tc2_done"], c + 1)
                if c >= 1:
                    act.wait_ge(sm["o_done"], c)
                nc.scalar.activation(ctxT[:, :], MB[:, 0:S], ACT.Copy).then_inc(sm["ctxT_ready"], 1)

            def x2_out(c):
                act.wait_ge(sm["o_done"], c + 1)
                if c >= 2:
                    act.wait_ge(sm["ff2_done"], c - 1)
                nc.scalar.activation(x2[:, c % 2, :, :], MC[:, 0:S].rearrange("p (t d) -> p t d", t=QT),
                                     ACT.Copy).then_inc(sm["x2_ready"], 1)

            def hT_out(c):
                act.wait_ge(sm["t2_done"], c + 1)
                if c >= 1:
                    act.wait_ge(sm["ff1_done"], 2 * c)
                nc.scalar.activation(hT[:, :], MB[:, S:2 * S], ACT.Identity, bias=col(BETA2), scale=col(G2)
                                     ).then_inc(sm["hT_ready"], 1)

            def th_out(c, j):
                act.wait_ge(sm["u_ready"], 2 * c + j + 1)
                if c >= 1:
                    act.wait_ge(sm["g_ready"], 2 * (c - 1) + j + 1)
                nc.scalar.activation(th[:, 2 * j:2 * j + 2, :], u[:, 2 * j:2 * j + 2, :], ACT.Tanh,
                                     scale=0.851).then_inc(sm["th_ready"], 1)

            def x3_out(c):
                act.wait_ge(sm["ff2_done"], c + 1)
                nc.scalar.activation(x3T[:, c, :], MA[:, 0:S], ACT.Identity, bias=col(B2)
                                     ).then_inc(sm["x3_ready"], 1)

            def hid_out(c):
                act.wait_ge(sm["dn_done"], c + 1)
                nc.scalar.activation(hid[:, c, :], MA[0:A, S:2 * S], ACT.Identity, bias=col(DOWNB, 1, A)
                                     ).then_inc(sm["hid_ready"], 1)

            def gelu(j):
                for b in GROUPS[j]:
                    act.wait_ge(sm["hid_ready"], b + 1)
                    nc.scalar.activation(ghid[:, b, :], hid[:, b, :], ACT.Gelu).then_inc(sm["ghid_ready"], 1)

            def eo_out(j):
                act.wait_ge(sm["eo_done"], j + 1)
                act.wait_ge(sm["ctx_done"], NG * B)
                for b in GROUPS[j]:
                    nc.scalar.activation(eoT[0:A, b, :], EB[0:A, (b % 2) * S:(b % 2 + 1) * S], ACT.Identity,
                                         bias=bsel[:, b:b + 1]).then_inc(sm["eo_ready"], 1)

            def norm3_out(j):
                act.wait_ge(sm["nmr_ready"], 1)
                for i in range(2 * QT * j, 2 * QT * (j + 1)):
                    t = i % (2 * QT)
                    nc.scalar.activation(y[:, i // QT, i % QT, :], UB[j][:, t * D:(t + 1) * D], ACT.Identity,
                                         bias=nmr3[:, i:i + 1], scale=nt3[:, 1, i:i + 1]
                                         ).then_inc(sm["y_norm"], 1)

            table = {0: [(x1T_out, -1)], 2: [(hT_out, 2), (qk_out, -1)],
                     6: [(lambda c: th_out(c, 0), 2)], 7: [(lambda c: th_out(c, 1), 2)],
                     9: [(mask_bias, -1)], 10: [(x3_out, 2), (ctxT_out, 1)],
                     12: [(x2_out, 1)], 13: [(hid_out, 2)]}
            y2, z = B - 2, B - 1
            drain = {(B, 3): [(hT_out, y2)],
                     (B, 5): [(gelu, 0), (th_out, y2, 0), (ctxT_out, z), (th_out, y2, 1), (eo_out, 0), (gelu, 1),
                              (x2_out, z), (eo_out, 1), (gelu, 2), (x3_out, y2), (hT_out, z), (eo_out, 2),
                              (hid_out, y2), (gelu, 3), (th_out, z, 0), (th_out, z, 1), (eo_out, 3),
                              (norm3_out, 0), (x3_out, z), (norm3_out, 1), (hid_out, z), (gelu, 4), (eo_out, 4)]}
            for n in STEPS:
                for h in range(H):
                    t = turning(n, h)
                    if t is not None:
                        probs(*t)
                    w = using(n, h)
                    if w is not None and w[1] % 2 == 1:
                        ctxA_out(w[0], w[1] // 2)
                    for f, back in table.get(h, []) if n < B else []:
                        c = item(n, back)
                        if c is not None:
                            f(c)
                    for f, *args in drain.get((n, h), []):
                        f(*args)

        @block.vector
        def _(dve):
            def stats1(t0, t1):
                for t in range(t0, t1):
                    if t % QT == 0:
                        dve.wait_ge(x_in[t // QT], 16)
                    nc.vector.bn_stats(st1[:, t, :], x_sb[:, t // QT, t % QT, :]).then_inc(sm["stats1"], 1)
                for t in range(t0, t1):
                    dve.wait_ge(sm["stats1"], t0 + t + 1)
                    nc.vector.bn_aggr(mv1[:, t, :], st1[:, t, :]).then_inc(sm["stats1"], 1)

            dve.wait_ge(sm["t_in"], 16)
            dve.wait_ge(sm["cols_in"], 16)
            nc.vector.tensor_copy(emb[:, 0, :], emb_i[:, :]).then_inc(sm["emb_x"], 1)
            dve.wait_ge(sm["emb_x"], 1)
            nc.vector.tensor_scalar(emb[:, 1, :], emb[:, 0, :], RESCALE / STEPS_T, None, ALU.mult
                                    ).then_inc(sm["emb_x"], 1)
            dve.wait_ge(sm["emb_x"], 2)
            nc.vector.tensor_scalar(emb[:, 0, :], emb[:, 1, :], col(FREQ), None, ALU.mult
                                    ).then_inc(sm["emb_x"], 1)
            dve.wait_ge(sm["emb_x"], 3)
            chain = [0]

            def link(ins, s="emb_silu"):
                chain[0] += 1
                ins.then_inc(sm[s], 1)
                dve.wait_ge(sm[s], chain[0])

            link(nc.vector.tensor_scalar(emb[:, 1, :], emb[:, 0, :], 1.0 / 6.283185307179586, col(PHASE),
                                         ALU.mult, ALU.add))
            link(nc.vector.tensor_scalar(emb[:, 2, :], emb[:, 1, :], ROUND, ROUND, ALU.add, ALU.subtract))
            for tau in (TAU1, TAU2, TAU3):
                link(nc.vector.scalar_tensor_tensor(emb[:, 0, :], emb[:, 2, :], -tau, emb[:, 0, :],
                                                    ALU.mult, ALU.add))
            nc.vector.tensor_scalar(emb[:, 1, :], col(PHASE).to_broadcast([P, B]), 6.283185307179586, None,
                                    ALU.mult).then_inc(sm["emb_x"], 1)
            dve.wait_ge(sm["emb_x"], 4)
            nc.vector.tensor_tensor(out=emb[:, 5, :], in0=emb[:, 0, :], in1=emb[:, 1, :], op=ALU.add
                                    ).then_inc(sm["emb_x"], 1)
            dve.wait_ge(sm["emb_x"], 5)
            nc.vector.tensor_scalar(emb[:, 2, :], emb[:, 5, :], 3.1415925, -3.1415925, ALU.min, ALU.max
                                    ).then_inc(sm["emb_x"], 1)

            def norm1(b):
                if b >= 2:
                    dve.wait_ge(sm["t1_done"], b - 1)
                dve.wait_ge(sm["nt1_step"], NSTEP * (1 if b == 0 else 2))
                for t in range(QT):
                    k = b * QT + t
                    last = nc.vector.tensor_scalar(z1[:, b % 2, t, :], x_sb[:, b, t, :], mv1[:, k, 0:1],
                                                   nt1[:, 1, k:k + 1], ALU.subtract, ALU.mult)
                last.then_inc(sm["z1_ready"], 1)

            stats1(0, QT)
            newton_seed(dve, mv1[:, 0:QT, 1], nt1[:, :, 0:QT], sm["stats1"], sm["y1_seed"], 2 * QT, 0, QT)
            dve.wait_ge(sm["y1_seed"], NSEED)
            newton_round(dve, nt1[:, :, 0:QT], sm["nt1_step"], 0)
            newton_round(dve, nt1[:, :, 0:QT], sm["nt1_step"], 1)
            dve.wait_ge(sm["emb_exp"], 1)
            link(nc.vector.tensor_scalar(emb[:, 5, :], emb[:, 4, :], 1.0, None, ALU.add))
            link(nc.vector.reciprocal(emb[:, 6, :], emb[:, 5, :]))
            link(nc.vector.tensor_tensor(out=emb[:, 7, :], in0=emb[:, 3, :], in1=emb[:, 6, :], op=ALU.mult))
            newton_round(dve, nt1[:, :, 0:QT], sm["nt1_step"], 2)
            norm1(0)
            dve.wait_ge(sm["ada_mm"], 1)
            nc.vector.tensor_scalar(ada[:, 0, :], MC[:, 0:B], col(BADA_S), 1.0, ALU.add, ALU.add
                                    ).then_inc(sm["ada_ready"], 1)
            nc.vector.tensor_scalar(ada[:, 1, :], MC[:, B:2 * B], col(BADA_H), None, ALU.add
                                    ).then_inc(sm["ada_ready"], 1)

            for w in range(2):
                dve.wait_ge(sm["qk_ready"], 2 * (w + 1))
                ins = nc.vector.tensor_tensor(out=qk_rest[:, w, :], in0=qkf[:, w, :], in1=parts[:, w, 0, :],
                                              op=ALU.subtract)
                ins.then_inc(sm["rest_ready"], 1)
                dve.wait_ge(sm["rest_ready"], w + 1)
                nc.vector.tensor_copy(parts[:, w, 1, :], qk_rest[:, w, :]).then_inc(sm["part2_ready"], 1)
                dve.wait_ge(sm["part2_ready"], w + 1)
                nc.vector.tensor_tensor(out=parts[:, w, 2, :], in0=qk_rest[:, w, :], in1=parts[:, w, 1, :],
                                        op=ALU.subtract).then_inc(sm["parts_ready"], 1)

            dve.wait_ge(sm["dom_in"], 16)
            E1 = A + 1
            dchain = [0]

            def dlink(ins):
                dchain[0] += 1
                ins.then_inc(sm["dom_ready"], 1)
                dve.wait_ge(sm["dom_ready"], dchain[0])

            dlink(nc.vector.tensor_copy(dom[:, 0, :], dom_i[:, :]))
            dlink(nc.vector.tensor_scalar(dom[:, 1, :], dom[:, 0, :], 0.0, float(NE - 1), ALU.max, ALU.min))
            dlink(nc.vector.tensor_tensor(out=dom[:, 2, :], in0=dom[:, 0, :], in1=dom[:, 1, :],
                                          op=ALU.is_equal))
            dlink(nc.vector.tensor_scalar(dom[:, 3, :], dom[:, 1, :], col(ECOL, 1, E1), None, ALU.is_equal))
            dlink(nc.vector.tensor_tensor(out=dom[:, 4, :], in0=dom[:, 3, :], in1=dom[:, 2, :], op=ALU.mult))
            dlink(nc.vector.tensor_scalar(dom[A:E1, 4, :], dom[A:E1, 2, :], -1.0, 1.0, ALU.mult, ALU.add))
            assert dchain[0] == 6
            stats1(QT, B * QT)
            newton_seed(dve, mv1[:, QT:, 1], nt1[:, :, QT:], sm["stats1"], sm["y1_seed"],
                        2 * B * QT, NSEED, (B - 1) * QT)
            newton_steps(dve, nt1[:, :, QT:], sm["y1_seed"], 2 * NSEED, sm["nt1_step"], ROUNDS)
            dve.wait_ge(sm["wsel_mm"], 1)
            nc.vector.tensor_copy(wsel[:, :, :].rearrange("a b o -> a o b"),
                                  MC[0:A, 0:A * B].rearrange("a (o b) -> a o b", b=B)
                                  ).then_inc(sm["wsel_ready"], 1)
            nc.vector.tensor_copy(bsel[:, :], MC[0:A, A * B:A * B + B]).then_inc(sm["wsel_ready"], 1)

            def scores(n, h):
                r = (n * NG + h // G) % RING
                dve.wait_ge(sm["scores_done"], H * n + h + 1)
                if h % G == 0:
                    dve.wait_ge(f_in[r], 16 * ((n * NG + h // G) // RING + 1))
                if h == 0 and n >= 2:
                    dve.wait_ge(sm["nan_ready"], n - 1)
                for t in range(QT):
                    last = nc.vector.tensor_tensor_reduce(
                        out=F[:, r, h % G, t, :], in0=SB[h % 2][:, t * S:(t + 1) * S], in1=F[:, r, h % G, t, :],
                        scale=1.0, scalar=-3.4e38, op0=ALU.add, op1=ALU.max,
                        accum_out=mx[:, n % 2, t, h:h + 1])
                last.then_inc(sm["scores_read"], 1)

            def center(n, h):
                r = (n * NG + h // G) % RING
                dve.wait_ge(sm["scores_read"], H * n + h + 1)
                for t in range(QT):
                    z = F[:, r, h % G, t, :]
                    last = nc.vector.tensor_scalar(z, z, mx[:, n % 2, t, h:h + 1], None, ALU.subtract)
                last.then_inc(sm["vec_centered"], 1)

            def v_out(b):
                dve.wait_ge(sm["vp_done"], b + 1)
                dve.wait_ge(sm["rows_in"], 16)
                dve.wait_ge(sm["ones_set"], 2)
                if b >= 2:
                    dve.wait_ge(sm["ctx_done"], NG * (b - 1))
                for t in range(QT):
                    last = nc.vector.tensor_tensor(
                        out=vaug[:, b % 2, t, :, 0:HD],
                        in0=MA[:, t * D:(t + 1) * D].rearrange("p (h d) -> p h d", h=H),
                        in1=rows_sb[:, 0, :].rearrange("p (h d) -> p h d", h=H), op=ALU.add)
                last.then_inc(sm["v_ready"], 1)

            def norm_ctx(c):
                dve.wait_ge(sm["tc_done"], 2 * (c + 1))
                dve.wait_ge(sm["nan_ready"], c + 1)
                if c >= 1:
                    dve.wait_ge(sm["tc2_done"], c)
                tb = [bank[:, :].rearrange("p (h e) -> p h e", h=H) for bank in turned_ctx_banks(c)]
                for t in range(QT):
                    last = nc.vector.tensor_tensor(out=csum[:, t, :], in0=tb[t][:, :, HD],
                                                   in1=nanfix[:, c % 2, t, :], op=ALU.add)
                last.then_inc(sm["rsum_fixed"], 1)
                dve.wait_ge(sm["rsum_fixed"], c + 1)
                nc.vector.reciprocal(csum[:, :, :], csum[:, :, :]).then_inc(sm["rsum_inv"], 1)
                dve.wait_ge(sm["rsum_inv"], c + 1)
                for t in range(QT):
                    last = nc.vector.tensor_tensor(
                        out=ctxn[:, t, :].rearrange("p (h d) -> p h d", h=H), in0=tb[t][:, :, 0:HD],
                        in1=csum[:, t, :].unsqueeze(2).to_broadcast([P, H, HD]), op=ALU.mult)
                last.then_inc(sm["ctxn_ready"], 1)

            def stats2(c):
                dve.wait_ge(sm["x2_ready"], c + 1)
                if c >= 1:
                    dve.wait_ge(sm["z2_ready"], c)
                for t in range(QT):
                    nc.vector.bn_stats(st2[:, t, :], x2[:, c % 2, t, :]).then_inc(sm["stats2"], 1)
                for t in range(QT):
                    dve.wait_ge(sm["stats2"], 2 * QT * c + QT + t)
                    nc.vector.bn_aggr(mv2[:, c % 2, t, :], st2[:, t, :]).then_inc(sm["stats2"], 1)
                newton_seed(dve, mv2[:, c % 2, :, 1], nt2, sm["stats2"], sm["y2_seed"], 2 * QT * (c + 1),
                            NSEED * c, QT)

            def round2(c, r):
                if r == 0:
                    dve.wait_ge(sm["y2_seed"], NSEED * (c + 1))
                newton_round(dve, nt2, sm["nt2_step"], ROUNDS * c + r)

            def norm2(c):
                dve.wait_ge(sm["nt2_step"], NSTEP * (c + 1))
                if c >= 1:
                    dve.wait_ge(sm["t2_done"], c)
                for t in range(QT):
                    last = nc.vector.tensor_scalar(z2[:, t, :], x2[:, c % 2, t, :], mv2[:, c % 2, t, 0:1],
                                                   nt2[:, 1, t:t + 1], ALU.subtract, ALU.mult)
                last.then_inc(sm["z2_ready"], 1)

            def u_out(c, j):
                dve.wait_ge(sm["ff1_done"], 2 * c + j + 1)
                if c >= 1:
                    dve.wait_ge(sm["ff2_done"], c)
                nc.vector.tensor_tensor(out=u[:, 2 * j:2 * j + 2, :],
                                        in0=(MB, MC)[j][:, :].rearrange("p (f s) -> p f s", f=2),
                                        in1=col(B1 + 2 * j, 2).unsqueeze(2).to_broadcast([P, 2, S]),
                                        op=ALU.add).then_inc(sm["u_ready"], 1)

            def halve_w2(n):
                dve.wait_ge(sm["w2_in"], 16)
                nc.vector.tensor_scalar(W2, W2, 0.5, None, ALU.mult).then_inc(sm["w2_halved"], 1)

            def g_out(c, j):
                dve.wait_ge(sm["th_ready"], 2 * c + j + 1)
                uu = u[:, 2 * j:2 * j + 2, :]
                nc.vector.scalar_tensor_tensor(uu, th[:, 2 * j:2 * j + 2, :], 1.0, uu, ALU.add, ALU.mult
                                               ).then_inc(sm["g_ready"], 1)

            def qk_part2(b):
                dve.wait_ge(sm["rest_ready"], b + 2)
                nc.vector.tensor_copy(parts[:, :, 1, :], qk_rest[:, :, :]).then_inc(sm["part2_ready"], 1)

            def norm3_stats(j):
                dve.wait_ge(sm["up_done"], j + 1)
                k0 = 2 * QT * j
                for t in range(2 * QT):
                    nc.vector.bn_stats(st3[:, k0 + t, :], UB[j][:, t * D:(t + 1) * D]).then_inc(sm["st3_step"], 1)
                for t in range(2 * QT):
                    dve.wait_ge(sm["st3_step"], 2 * k0 + t + 1)
                    nc.vector.bn_aggr(mv3[:, k0 + t, :], st3[:, k0 + t, :]).then_inc(sm["st3_step"], 1)

            def norm3_inv(n):
                m = QT * NE3
                newton_seed(dve, mv3[:, 0:m, 1], nt3[:, :, 0:m], sm["st3_step"], sm["y3_seed"], 2 * m, 0, m)
                newton_steps(dve, nt3[:, :, 0:m], sm["y3_seed"], NSEED, sm["nt3_step"], 0)
                dve.wait_ge(sm["nt3_step"], NSTEP)
                nc.vector.scalar_tensor_tensor(nmr3[:, 0:m], mv3[:, 0:m, 0], -1.0, nt3[:, 1, 0:m],
                                               ALU.mult, ALU.mult).then_inc(sm["nmr_ready"], 1)

            def norm3_out(j):
                dve.wait_ge(sm["nmr_ready"], 1)
                for i in range(2 * QT * j, 2 * QT * (j + 1)):
                    t = i % (2 * QT)
                    nc.vector.tensor_scalar(y[:, i // QT, i % QT, :], UB[j][:, t * D:(t + 1) * D], mv3[:, i, 0:1],
                                            nt3[:, 1, i:i + 1], ALU.subtract, ALU.mult
                                            ).then_inc(sm["y_norm_v"], 1)

            def norm3(q):
                dve.wait_ge(sm["up_done"], q + 1)
                r = q - NE3 // 2 + 1
                k0 = QT * GROUPS[q][0]
                tiles = range(k0, k0 + QT * len(GROUPS[q]))
                nt = nt3[:, :, k0:tiles.stop]

                def bank(i):
                    return UB[q][:, (i % (2 * QT)) * D:(i % (2 * QT) + 1) * D]

                for i in tiles:
                    nc.vector.bn_stats(st3[:, i, :], bank(i)).then_inc(sm["st3_step"], 1)
                for i in tiles:
                    dve.wait_ge(sm["st3_step"], k0 + i + 1)
                    nc.vector.bn_aggr(mv3[:, i, :], st3[:, i, :]).then_inc(sm["st3_step"], 1)
                newton_seed(dve, mv3[:, k0:tiles.stop, 1], nt, sm["st3_step"], sm["y3_seed"], 2 * tiles.stop,
                            NSEED * r, len(tiles))
                for i in tiles:
                    nc.vector.scalar_tensor_tensor(y[:, i // QT, i % QT, :], bank(i), mv3[:, i, 0:1],
                                                   rows_sb[:, 1, :], ALU.subtract, ALU.mult
                                                   ).then_inc(sm["last_step"], 1)
                newton_steps(dve, nt, sm["y3_seed"], NSEED * (r + 1), sm["nt3_step"], ROUNDS * r)
                dve.wait_ge(sm["nt3_step"], NSTEP * (r + 1))
                for i in tiles:
                    dve.wait_ge(sm["last_step"], i - QT * NE3 + 1)
                    yt = y[:, i // QT, i % QT, :]
                    nc.vector.scalar_tensor_tensor(yt, yt, nt3[:, 1, i:i + 1], rows_sb[:, 2, :],
                                                   ALU.mult, ALU.add).then_inc(sm["last_ready"], 1)

            table = {0: [(norm2, 2)], 4: [(lambda c: u_out(c, 0), 2)],
                     5: [(lambda c: u_out(c, 1), 2), (qk_part2, -1)],
                     6: [(v_out, 0)], 7: [(lambda c: g_out(c, 0), 2)], 8: [(lambda c: g_out(c, 1), 2)],
                     9: [(norm_ctx, 1)], 12: [(stats2, 1), (norm1, -2)], 13: [(lambda c: round2(c, 0), 1)],
                     14: [(lambda c: round2(c, 1), 1)], 15: [(lambda c: round2(c, 2), 1)]}
            y2, z = B - 2, B - 1
            drain = {(0, 15): [(halve_w2, 0)],
                     (B, 0): [(norm2, y2), (u_out, y2, 0), (norm_ctx, z), (u_out, y2, 1), (g_out, y2, 0),
                              (g_out, y2, 1), (stats2, z), (round2, z, 0), (round2, z, 1), (round2, z, 2),
                              (norm2, z), (norm3_stats, 0), (norm3_stats, 1), (u_out, z, 0), (u_out, z, 1),
                              (g_out, z, 0), (g_out, z, 1), (norm3_stats, 2), (norm3_inv, 0), (norm3_out, 2),
                              (norm3, 3), (norm3, 4)]}
            for n in STEPS:
                for h in range(H):
                    c = item(n, 0)
                    if c is not None:
                        scores(c, h)
                        if h - 1 in VHEADS:
                            center(c, h - 1)
                    for f, back in table.get(h, []) if n < B else []:
                        c = item(n, back)
                        if c is not None and not (f is qk_part2 and c == 0):
                            f(c)
                    for f, *args in drain.get((n, h), []):
                        f(*args)

        @block.tensor
        def _(pe):
            mm = nc.tensor.matmul

            def turn(dst, src, start=True, stop=True):
                return mm(dst, src, idf[:, :], start=start, stop=stop, is_transpose=True)

            def turn_z1(b):
                pe.wait_ge(sm["z1_ready"], b + 1)
                if b == 0:
                    pe.wait_ge(sm["idf_in"], 16)
                if b >= 2:
                    pe.wait_ge(sm["v_ready"], b - 1)
                if b >= 4:
                    pe.wait_ge(sm["hid_ready"], b - 3)
                for t in range(QT):
                    last = turn(MA[:, t * P:(t + 1) * P], z1[:, b % 2, t, :])
                last.then_inc(sm["t1_done"], 1)

            def project_qk(b):
                pe.wait_ge(sm["x1T_ready"], b + 1)
                mm(MA[:, 0:S], WQ, x1T[:, b, :], start=True, stop=True)
                mm(MA[:, S:2 * S], WK, x1T[:, b, :], start=True, stop=True).then_inc(sm["qkp_done"], 1)

            def project_v(b):
                pe.wait_ge(sm["qk_ready"], 4 * min(b + 2, B))
                for t in range(QT):
                    last = mm(MA[:, t * D:(t + 1) * D], x1T[:, b, t * P:(t + 1) * P], WV, start=True, stop=True)
                last.then_inc(sm["vp_done"], 1)

            def score(n, h):
                bank = SB[h % 2]
                if h == 0:
                    pe.wait_ge(sm["maskb_ready"], n + 1)
                    pe.wait_ge(q_in[n % 2], 16 * (n // 2 + 1))
                    pe.wait_ge(k_in[n % 2], 16 * NPARTS * (n // 2 + 1))
                    if n == 0:
                        pe.wait_ge(sm["idb_in"], 16)
                if H * n + h >= 2:
                    pe.wait_ge(sm["scores_read"], H * n + h - 1)
                mm(bank[:, :], idb[:, :], maskb[:, n % 2, :, :].rearrange("p t s -> p (t s)"),
                   start=True, stop=False)
                for t in range(QT):
                    last = mm(bank[:, t * S:(t + 1) * S], qstack[:, n % 2, h, t * P:(t + 1) * P],
                              kstack[:, n % 2, h, :], start=False, stop=(t == QT - 1))
                last.then_inc(sm["scores_done"], 1)

            def turn_scores(c, h):
                k = H * c + h
                bank = ZB[k % 2]
                mine = [i for i in range(h + 1) if (i in VHEADS) == (h in VHEADS)]
                if h in VHEADS:
                    pe.wait_ge(sm["vec_centered"], len(VHEADS) * c + len(mine))
                else:
                    pe.wait_ge(sm["pool_centered"], (H - len(VHEADS)) * c + len(mine))
                if k >= 2:
                    pe.wait_ge(sm["probs_ready"], k - 1)
                r = (c * NG + h // G) % RING
                for kt in range(QT):
                    for t in range(QT):
                        last = turn(bank[:, kt * S + t * P:kt * S + (t + 1) * P],
                                    F[:, r, h % G, t, kt * P:(kt + 1) * P])
                last.then_inc(sm["turned"], 1)

            def context(c, g):
                pe.wait_ge(sm["probs_ready"], H * c + G * (g + 1))
                if g == 0:
                    pe.wait_ge(sm["v_ready"], c + 1)
                if g % 2 == 0 and NG * c + g >= 2:
                    pe.wait_ge(sm["ctxA_ready"], (NG * c + g) // 2)
                for kt in range(QT):
                    for j in range(G):
                        h = G * g + j
                        last = mm(CB[32 * j:32 * j + 32, (g % 2) * S:(g % 2 + 1) * S],
                                  vaug[:, c % 2, kt, h, :], PT[:, (H * c + h) % NPT, kt, :],
                                  start=(kt == 0), stop=(kt == QT - 1))
                last.then_inc(sm["ctx_done"], 1)

            def turn_ctx(c):
                pe.wait_ge(sm["ctxA_ready"], 2 * (c + 1))
                if c == 0:
                    pe.wait_ge(sm["wsel_ready"], 2)
                else:
                    if c < B - 1:
                        pe.wait_ge(sm["u_ready"], 2 * c)
                    else:
                        pe.wait_ge(sm["scores_read"], H * B)
                for t in range(QT):
                    for g in range(NG):
                        last = turn(turned_ctx_banks(c)[t][:, g * P:(g + 1) * P], ctxA[:, g, t * P:(t + 1) * P])
                    last.then_inc(sm["tc_done"], 1)

            def turn_ctxn(c):
                pe.wait_ge(sm["ctxn_ready"], c + 1)
                if c == B - 1:
                    pe.wait_ge(sm["u_ready"], 2 * c - 1)
                for t in range(QT):
                    last = turn(MB[:, t * P:(t + 1) * P], ctxn[:, t, :])
                last.then_inc(sm["tc2_done"], 1)

            def out_project(c):
                pe.wait_ge(sm["ctxT_ready"], c + 1)
                if c == B - 1:
                    pe.wait_ge(sm["u_ready"], 2 * c)
                if c == 0:
                    pe.wait_ge(sm["bo_in"], 16)
                    pe.wait_ge(sm["pads_set"], 1)
                for t in range(QT):
                    o = MC[:, t * D:(t + 1) * D]
                    mm(o, ctxT[:, t * P:(t + 1) * P], WO, start=True, stop=False)
                    mm(o, ones_row[:, :], bo_sb[:, :], start=False, stop=False)
                    last = turn(o, x1T[:, c, t * P:(t + 1) * P], start=False, stop=True)
                last.then_inc(sm["o_done"], 1)

            def turn_z2(c):
                pe.wait_ge(sm["z2_ready"], c + 1)
                for t in range(QT):
                    last = turn(MB[:, S + t * P:S + (t + 1) * P], z2[:, t, :])
                last.then_inc(sm["t2_done"], 1)

            def ff1(c, j):
                if j == 0:
                    pe.wait_ge(sm["hT_ready"], c + 1)
                else:
                    pe.wait_ge(sm["x2_ready"], c + 1)
                for i in range(2):
                    f = 2 * j + i
                    last = mm((MB, MC)[j][:, i * S:(i + 1) * S], W1[:, f * P:(f + 1) * P], hT[:, :],
                              start=True, stop=True)
                last.then_inc(sm["ff1_done"], 1)

            def ff2(c):
                pe.wait_ge(sm["g_ready"], 2 * (c + 1))
                if c == 0:
                    pe.wait_ge(sm["w2_halved"], 1)
                pe.wait_ge(sm["v_ready"], min(c + 3, B))
                for f in range(FF):
                    mm(MA[:, 0:S], W2[:, f * P:(f + 1) * P], u[:, f, :], start=(f == 0), stop=False)
                for t in range(QT):
                    last = turn(MA[:, t * P:(t + 1) * P], x2[:, c % 2, t, :], start=False, stop=(t == QT - 1))
                last.then_inc(sm["ff2_done"], 1)

            def down_project(c):
                pe.wait_ge(sm["x3_ready"], c + 1)
                if c == 0:
                    pe.wait_ge(sm["down_in"], 16)
                mm(MA[0:A, S:2 * S], down_sb[:, :], x3T[:, c, :], start=True, stop=True).then_inc(sm["dn_done"], 1)

            pe.wait_ge(sm["w_in"], 16)
            pe.wait_ge(sm["emb_silu"], 8)
            mm(MC[:, 0:B], WADA[:, 0:D], emb[:, 7, :], start=True, stop=True)
            mm(MC[:, B:2 * B], WADA[:, D:2 * D], emb[:, 7, :], start=True, stop=True).then_inc(sm["ada_mm"], 1)
            turn_z1(0)
            project_qk(0)
            pe.wait_ge(sm["expert_in"], 16)
            pe.wait_ge(sm["dom_ready"], 6)
            pe.wait_ge(sm["ada_ready"], 2)
            for o in range(A):
                mm(MC[0:A, o * B:(o + 1) * B], expert_sb[:, o * A:(o + 1) * A], dom[:, 4, :],
                   start=True, stop=True)
            mm(MC[0:A, A * B:A * B + B], expert_sb[:, A * A:A * A + A], dom[:, 4, :], start=True, stop=False)
            mm(MC[0:A, A * B:A * B + B], expert_sb[:, A * A + A:A * A + 2 * A], dom[:, 3, :],
               start=False, stop=True).then_inc(sm["wsel_mm"], 1)

            def expert(j):
                if j == 0:
                    pe.wait_ge(sm["probs_ready"], H * B)
                else:
                    pe.wait_ge(sm["eo_ready"], GROUPS[j][0])
                for b in GROUPS[j]:
                    pe.wait_ge(sm["ghid_ready"], b + 1)
                    last = mm(EB[0:A, (b % 2) * S:(b % 2 + 1) * S], wsel[:, b, :], ghid[:, b, :],
                              start=True, stop=True)
                last.then_inc(sm["eo_done"], 1)

            def up_project(j):
                if j == 0:
                    pe.wait_ge(sm["up_in"], 16)
                    pe.wait_ge(sm["pads_set"], 2)
                    pe.wait_ge(sm["probs_ready"], H * B)
                if j == 1:
                    pe.wait_ge(sm["ctxn_ready"], B)
                if j == 3:
                    pe.wait_ge(sm["ctxA_ready"], 2 * B)
                if j == 4:
                    pe.wait_ge(sm["u_ready"], 2 * B)
                for b in GROUPS[j]:
                    pe.wait_ge(sm["eo_ready"], b + 1)
                    for t in range(QT):
                        o = UB[j][:, (b % 2 * QT + t) * D:(b % 2 * QT + t + 1) * D]
                        mm(o, eoT[:, b, t * P:(t + 1) * P], up_sb[:, :], start=True, stop=False)
                        last = turn(o, x3T[:, b, t * P:(t + 1) * P], start=False, stop=True)
                last.then_inc(sm["up_done"], 1)

            table = {0: [(turn_z1, -1)], 2: [(turn_z2, 2), (project_qk, -1)], 4: [(lambda c: ff1(c, 0), 2)],
                     5: [(project_v, 0), (lambda c: ff1(c, 1), 2)], 8: [(turn_ctx, 1)],
                     10: [(ff2, 2), (turn_ctxn, 1)], 12: [(out_project, 1)], 13: [(down_project, 2)]}
            y2, z = B - 2, B - 1
            drain = {(B, 3): [(turn_z2, y2)],
                     (B, 5): [(ff1, y2, 0), (turn_ctx, z), (ff1, y2, 1), (turn_ctxn, z), (expert, 0),
                              (out_project, z), (up_project, 0), (expert, 1), (ff2, y2), (up_project, 1),
                              (turn_z2, z), (expert, 2), (down_project, y2), (ff1, z, 0), (ff1, z, 1),
                              (expert, 3), (up_project, 2), (up_project, 3), (ff2, z), (down_project, z),
                              (expert, 4), (up_project, 4)]}
            for n in STEPS:
                for h in range(H):
                    c = item(n, 0)
                    if c is not None:
                        score(c, h)
                    t = turning(n, h)
                    if t is not None:
                        turn_scores(*t)
                    w = using(n, h)
                    if w is not None:
                        context(*w)
                    for f, back in table.get(h, []) if n < B else []:
                        c = item(n, back)
                        if c is not None and not (f in (turn_z1, project_qk) and c == 0):
                            f(c)
                    for f, *args in drain.get((n, h), []):
                        f(*args)


def kernel(**inputs):
    import math
    import ml_dtypes
    import numpy as np
    import concourse.bacc as bacc
    from concourse import mybir
    from concourse.bass_utils import run_bass_kernel_spmd

    a = {k: np.asarray(v) for k, v in inputs.items()}
    f32 = np.float32
    B, S, D = a["x"].shape
    H = a["fside_Bx16xSxS_0"].shape[1]
    A = a["L1_cond_down_W"].shape[0]
    NE = a["L1_cond_expert_W"].shape[0]
    P, half = 128, D // 2
    freqs = np.exp(np.arange(half, dtype=f32) * f32(-math.log(10000.0) / (half - 1))).astype(f32)
    freq = np.concatenate([freqs, freqs])
    phase = np.concatenate([np.zeros(half, f32), np.full(half, 0.25, f32)])
    ecol = np.full(P, -1.0, f32)
    ecol[:NE] = np.arange(NE)
    L0 = lambda n: a["L0_cond_" + n]
    L1 = lambda n: a["L1_cond_" + n]
    w2 = L0("W2").reshape(4, P, D).transpose(1, 0, 2).reshape(P, 4 * D)
    by_dim = lambda v: v.reshape(*v.shape[:-1], H, D // H).swapaxes(-1, -2).reshape(v.shape)
    wts = np.concatenate([by_dim(L0("Wq")), by_dim(L0("Wk")), L0("Wv"), L0("Wo"), L0("W_ada"), L0("W1"), w2], axis=1)
    downb = np.zeros(P, f32)
    downb[:A] = L1("down_b")
    cols = np.stack([L0("b_ada")[:D], L0("b_ada")[D:], by_dim(L0("bq")), by_dim(L0("bk")), L0("g2"), L0("beta2"), L0("b2"),
                     freq, phase, ecol, downb, *L0("b1").reshape(4, P)], axis=1)
    rows = np.stack([L0("bv"), L1("ln_gamma"), L1("ln_beta")])
    expert = np.zeros((A + 1, A * A + 2 * A), f32)
    expert[:NE, :A * A] = L1("expert_W").reshape(NE, A * A)
    expert[A, :A * A] = np.eye(A, dtype=f32).reshape(-1)
    expert[:NE, A * A:A * A + A] = L1("expert_b")
    expert[:NE, A * A + A:] = L1("domain_emb")
    up = np.concatenate([L1("up_W").T, L1("up_b")[None, :]], axis=0)
    arrays = {
        "x": a["x"], "tstep": a["itok_B_34_63"], "fside": a["fside_Bx16xSxS_0"], "domain": a["itok_B_0_15"],
        "mask": a["mask_Bx1xSxS_bk0"], "wts": wts, "cols": cols, "rows": rows,
        "bo": L0("bo")[None, :], "down": L1("down_W").T, "up": up, "expert": expert,
        "identf": np.eye(P, dtype=f32), "identb": np.eye(P, dtype=f32).astype(ml_dtypes.bfloat16),
    }
    nc = bacc.Bacc("TRN2", target_bir_lowering=False, num_devices=1)
    named, args = {}, []
    for name, v in arrays.items():
        v = np.ascontiguousarray(v)
        named[f"in_{name}"] = v
        args.append(nc.dram_tensor(f"in_{name}", v.shape, mybir.dt.from_np(v.dtype), kind="ExternalInput").ap())
    args.append(nc.dram_tensor("out_0", (B, S, D), mybir.dt.float32, kind="ExternalOutput").ap())
    cond_seq_kernel(nc, *args)
    r = run_bass_kernel_spmd(nc, [named], core_ids=[0])
    return r.results[0]["out_0"]
```
